# Optimizing a Trainium2 kernel written in Bass

```python
import numpy as np
import jax
import jax.numpy as jnp

def _softmax(x, axis=-1):
    return jax.nn.softmax(x, axis=axis)

def _gelu(x):
    return jax.nn.gelu(x, approximate=True)

def _silu(x):
    return jax.nn.silu(x)

def _sigmoid(x):
    return jax.nn.sigmoid(x)

def _layernorm(x, axis=-1, eps=1e-05):
    m = jnp.mean(x, axis=axis, keepdims=True)
    v = jnp.var(x, axis=axis, keepdims=True)
    return (x - m) / jnp.sqrt(v + eps)

def _scatter_add(tgt, idx, src, axis=0):
    return tgt.at[idx].add(src)

def _segment_sum(src, seg, n):
    return jax.ops.segment_sum(src, seg, n)
kernel_name = 'mk_cond_resid_d4_seqx_r2_a385f0'

def setup_inputs(seed: int=0):
    np.random.seed(seed)
    _w = jnp.asarray

    def _rec_inputs():
        import jax
        import jax.numpy as jnp
        _rk = jax.random.key(seed)
        x = 0.5 + 0.2887 * jax.random.normal(jax.random.fold_in(_rk, 1), (16, 512, 512), jnp.float32)
        _lenS = 512 - jax.random.randint(jax.random.fold_in(_rk, 7), (16,), 0, max(1, 512 // 4) + 1, jnp.int32)
        _lenS2 = 512 - jax.random.randint(jax.random.fold_in(_rk, 8), (16,), 0, max(1, 512 // 4) + 1, jnp.int32)
        condB_zX = jax.random.uniform(jax.random.fold_in(_rk, 11), (16,), jnp.float32, 0.0, 0.983423)
        condB_zY = jax.random.uniform(jax.random.fold_in(_rk, 12), (16,), jnp.float32, 0.0, 0.979075)
        condB_zR = jax.random.uniform(jax.random.fold_in(_rk, 13), (16,), jnp.float32, 0.0, 0.9968)
        itok_B_0_6 = jax.random.randint(jax.random.fold_in(_rk, 14), (16,), 0, 7, jnp.int32)
        itok_B_0_8 = jax.random.randint(jax.random.fold_in(_rk, 15), (16,), 0, 9, jnp.int32)
        condB_alphaparams = -2 + 1 * jax.random.normal(jax.random.fold_in(_rk, 16), (16,), jnp.float32)
        return (x, condB_zX, condB_zY, condB_zR, itok_B_0_6, itok_B_0_8, condB_alphaparams)
    x, condB_zX, condB_zY, condB_zR, itok_B_0_6, itok_B_0_8, condB_alphaparams = _rec_inputs()

    def _L0_cond_setup():
        import jax, jax.numpy as jnp
        import numpy as np
        key = jax.random.key(seed)
        k1, k2, k3, k4 = jax.random.split(key, 4)
        B, H, W = (64, 512, 512)
        return {'y': jax.random.uniform(k1, (B, H, W), dtype=jnp.float32), 'zX': jax.random.uniform(k2, (B, 1), dtype=jnp.float32), 'zY': jax.random.uniform(k3, (B, 1), dtype=jnp.float32), 'zR': jax.random.uniform(k4, (B, 1), dtype=jnp.float32), 'dx': 1, 'dy': 1}
    _L0_cond_all = _L0_cond_setup()
    _L0_cond_in = {k: v for k, v in _L0_cond_all.items() if k in ()}
    del _L0_cond_all

    def _L1_cond_setup():
        import jax, jax.numpy as jnp
        import numpy as np
        N_PROFILES = 8
        HIDDEN = 512
        BOTTLENECK = 128
        EPS = 1e-05
        key = jax.random.key(seed)
        ks = jax.random.split(key, 8)
        B, S, H, K, P = (16, 1024, HIDDEN, BOTTLENECK, N_PROFILES)
        down_w = jax.random.normal(ks[0], (P, H, K), dtype=jnp.float32) * (1.0 / np.sqrt(H))
        down_b = jax.random.normal(ks[1], (P, K), dtype=jnp.float32) * 0.01
        up_w = jax.random.normal(ks[2], (P, K, H), dtype=jnp.float32) * (1.0 / np.sqrt(K))
        up_b = jax.random.normal(ks[3], (P, H), dtype=jnp.float32) * 0.01
        ln_g = jnp.ones((P, H), dtype=jnp.float32)
        ln_b = jnp.zeros((P, H), dtype=jnp.float32)
        hidden = jax.random.normal(ks[4], (B, S, H), dtype=jnp.float32)
        profile_ids = jax.random.randint(ks[5], (B,), 0, P)
        return {'hidden': hidden, 'profile_ids': profile_ids, 'down_w': down_w, 'down_b': down_b, 'up_w': up_w, 'up_b': up_b, 'ln_g': ln_g, 'ln_b': ln_b}
    _L1_cond_all = _L1_cond_setup()
    _L1_cond_in = {k: v for k, v in _L1_cond_all.items() if k in ('down_w', 'down_b', 'up_w', 'up_b', 'ln_g', 'ln_b')}
    del _L1_cond_all

    def _L2_cond_setup():
        import jax, jax.numpy as jnp
        import numpy as np
        LN_EPS = 1e-05
        key = jax.random.key(seed)
        ks = jax.random.split(key, 8)
        B, S, H, A, L = (32, 1024, 512, 128, 10)
        return {'hidden_states': jax.random.normal(ks[0], (B, S, H), dtype=jnp.float32), 'language_ids': jax.random.randint(ks[1], (B,), 0, L, dtype=jnp.int64), 'W1': jax.random.normal(ks[2], (L, H, A), dtype=jnp.float32) * (1.0 / np.sqrt(H)), 'b1': jnp.zeros((L, A), dtype=jnp.float32), 'W2': jax.random.normal(ks[3], (L, A, H), dtype=jnp.float32) * (1.0 / np.sqrt(A)), 'b2': jnp.zeros((L, H), dtype=jnp.float32), 'gamma': jnp.ones((L, H), dtype=jnp.float32), 'beta': jnp.zeros((L, H), dtype=jnp.float32)}
    _L2_cond_all = _L2_cond_setup()
    _L2_cond_in = {k: v for k, v in _L2_cond_all.items() if k in ('W1', 'b1', 'W2', 'b2', 'gamma', 'beta')}
    del _L2_cond_all

    def _L3_cond_setup():
        import jax, jax.numpy as jnp
        import numpy as np
        D = 512
        L = 32
        B = 512

        def _ln(x, g, b, eps=1e-05):
            m = jnp.mean(x, axis=-1, keepdims=True)
            v = jnp.mean((x - m) ** 2, axis=-1, keepdims=True)
            return (x - m) / jnp.sqrt(v + eps) * g + b
        key = jax.random.key(seed)
        ks = jax.random.split(key, 6)
        s1 = 1.0 / np.sqrt(D)
        s2 = 1.0 / np.sqrt(4 * D)
        s3 = 1.0 / np.sqrt(2 * D)
        return {'z': jax.random.normal(ks[0], (L, B, D), jnp.float32), 's_init': jax.random.normal(ks[1], (B, D), jnp.float32), 'alpha_params': jnp.full((L,), -2.0, jnp.float32), 'W1': jax.random.uniform(ks[2], (D, 4 * D), jnp.float32, -s1, s1), 'b1': jax.random.uniform(ks[3], (4 * D,), jnp.float32, -s1, s1), 'g1': jnp.ones((4 * D,), jnp.float32), 'be1': jnp.zeros((4 * D,), jnp.float32), 'W2': jax.random.uniform(ks[4], (4 * D, D), jnp.float32, -s2, s2), 'b2': jax.random.uniform(ks[5], (D,), jnp.float32, -s2, s2), 'g2': jnp.ones((D,), jnp.float32), 'be2': jnp.zeros((D,), jnp.float32), 'Wt': jax.random.uniform(jax.random.fold_in(key, 7), (2 * D, D), jnp.float32, -s3, s3), 'bt': jax.random.uniform(jax.random.fold_in(key, 8), (D,), jnp.float32, -s3, s3), 'gt': jnp.ones((D,), jnp.float32), 'bet': jnp.zeros((D,), jnp.float32), 'tree_checkpoint': 4}
    _L3_cond_all = _L3_cond_setup()
    _L3_cond_in = {k: v for k, v in _L3_cond_all.items() if k in ('s_init', 'W1', 'b1', 'g1', 'be1', 'W2', 'b2', 'g2', 'be2', 'Wt', 'bt', 'gt', 'bet')}
    del _L3_cond_all
    return {'x': x, 'condB_zX': condB_zX, 'condB_zY': condB_zY, 'condB_zR': condB_zR, 'itok_B_0_6': itok_B_0_6, 'itok_B_0_8': itok_B_0_8, 'condB_alphaparams': condB_alphaparams, 'L1_cond_down_w': _L1_cond_in['down_w'], 'L1_cond_down_b': _L1_cond_in['down_b'], 'L1_cond_up_w': _L1_cond_in['up_w'], 'L1_cond_up_b': _L1_cond_in['up_b'], 'L1_cond_ln_g': _L1_cond_in['ln_g'], 'L1_cond_ln_b': _L1_cond_in['ln_b'], 'L2_cond_W1': _L2_cond_in['W1'], 'L2_cond_b1': _L2_cond_in['b1'], 'L2_cond_W2': _L2_cond_in['W2'], 'L2_cond_b2': _L2_cond_in['b2'], 'L2_cond_gamma': _L2_cond_in['gamma'], 'L2_cond_beta': _L2_cond_in['beta'], 'L3_cond_s_init': _L3_cond_in['s_init'], 'L3_cond_W1': _L3_cond_in['W1'], 'L3_cond_b1': _L3_cond_in['b1'], 'L3_cond_g1': _L3_cond_in['g1'], 'L3_cond_be1': _L3_cond_in['be1'], 'L3_cond_W2': _L3_cond_in['W2'], 'L3_cond_b2': _L3_cond_in['b2'], 'L3_cond_g2': _L3_cond_in['g2'], 'L3_cond_be2': _L3_cond_in['be2'], 'L3_cond_Wt': _L3_cond_in['Wt'], 'L3_cond_bt': _L3_cond_in['bt'], 'L3_cond_gt': _L3_cond_in['gt'], 'L3_cond_bet': _L3_cond_in['bet']}

def reference(x, condB_zX, condB_zY, condB_zR, itok_B_0_6, itok_B_0_8, condB_alphaparams, L1_cond_down_w, L1_cond_down_b, L1_cond_up_w, L1_cond_up_b, L1_cond_ln_g, L1_cond_ln_b, L2_cond_W1, L2_cond_b1, L2_cond_W2, L2_cond_b2, L2_cond_gamma, L2_cond_beta, L3_cond_s_init, L3_cond_W1, L3_cond_b1, L3_cond_g1, L3_cond_be1, L3_cond_W2, L3_cond_b2, L3_cond_g2, L3_cond_be2, L3_cond_Wt, L3_cond_bt, L3_cond_gt, L3_cond_bet):
    import jax
    import jax.numpy as jnp

    def _L0_cond_ref(y, zX, zY, zR, dx, dy):
        import jax, jax.numpy as jnp
        import numpy as np
        yp_x = jnp.pad(y, ((0, 0), (0, 0), (1, 1)), mode='reflect')
        lap_x = (yp_x[:, :, :-2] - 2.0 * y + yp_x[:, :, 2:]) / (dx * dx)
        yp_y = jnp.pad(y, ((0, 0), (1, 1), (0, 0)), mode='reflect')
        lap_y = (yp_y[:, :-2, :] - 2.0 * y + yp_y[:, 2:, :]) / (dy * dy)
        du_dt = zX[:, :, None] * lap_x + zY[:, :, None] * lap_y + zR[:, :, None] * y * (1.0 - y)
        return du_dt

    def _L1_cond_ref(hidden, profile_ids, down_w, down_b, up_w, up_b, ln_g, ln_b):
        import jax, jax.numpy as jnp
        import numpy as np
        N_PROFILES = 8
        HIDDEN = 512
        BOTTLENECK = 128
        EPS = 1e-05
        Wd = down_w[profile_ids]
        bd = down_b[profile_ids][:, None]
        Wu = up_w[profile_ids]
        bu = up_b[profile_ids][:, None]
        g = ln_g[profile_ids][:, None]
        b = ln_b[profile_ids][:, None]
        z = jax.nn.relu(jnp.einsum('bsh,bhk->bsk', hidden, Wd) + bd)
        y = hidden + jnp.einsum('bsk,bkh->bsh', z, Wu) + bu
        mu = jnp.mean(y, axis=-1, keepdims=True)
        var = jnp.mean(jnp.square(y - mu), axis=-1, keepdims=True)
        return (y - mu) * jax.lax.rsqrt(var + EPS) * g + b

    def _L2_cond_ref(hidden_states, language_ids, W1, b1, W2, b2, gamma, beta):
        import jax, jax.numpy as jnp
        import numpy as np
        LN_EPS = 1e-05
        w1 = W1[language_ids]
        w2 = W2[language_ids]
        h = jnp.einsum('bsh,bha->bsa', hidden_states, w1) + b1[language_ids][:, None, :]
        h = jax.nn.relu(h)
        adapted = jnp.einsum('bsa,bah->bsh', h, w2) + b2[language_ids][:, None, :]
        x = hidden_states + adapted
        mean = jnp.mean(x, axis=-1, keepdims=True)
        var = jnp.mean(jnp.square(x - mean), axis=-1, keepdims=True)
        normed = (x - mean) * jax.lax.rsqrt(var + LN_EPS)
        return normed * gamma[language_ids][:, None, :] + beta[language_ids][:, None, :]

    def _L3_cond_ref(z, s_init, alpha_params, W1, b1, g1, be1, W2, b2, g2, be2, Wt, bt, gt, bet, tree_checkpoint):
        import jax, jax.numpy as jnp
        import numpy as np
        D = 512
        L = 32
        B = 512

        def _ln(x, g, b, eps=1e-05):
            m = jnp.mean(x, axis=-1, keepdims=True)
            v = jnp.mean((x - m) ** 2, axis=-1, keepdims=True)
            return (x - m) / jnp.sqrt(v + eps) * g + b
        h = jax.nn.gelu(jnp.einsum('lbd,df->lbf', z, W1) + b1, approximate=False)
        h = _ln(h, g1, be1)
        phi = _ln(jnp.einsum('lbf,fd->lbd', h, W2) + b2, g2, be2)
        alphas = jax.nn.sigmoid(alpha_params)
        tc = int(tree_checkpoint)
        s = s_init
        s_list = []
        for l in range(z.shape[0]):
            a = alphas[l]
            s = (1.0 - a) * s + a * phi[l]
            if tc > 0 and (l + 1) % tc == 0:
                ckpt = s_list[-(tc // 2)] if len(s_list) >= tc // 2 else s_init
                comb = jnp.concatenate([s, ckpt], axis=-1)
                s = _ln(jax.nn.gelu(comb @ Wt + bt, approximate=False), gt, bet)
            s_list.append(s)
        return jnp.stack(s_list, axis=0)
    x = x + _L0_cond_ref(x, condB_zX[:, None], condB_zY[:, None], condB_zR[:, None], 1, 1)
    x = x + _L1_cond_ref(x, itok_B_0_6, L1_cond_down_w, L1_cond_down_b, L1_cond_up_w, L1_cond_up_b, L1_cond_ln_g, L1_cond_ln_b)
    x = x + _L2_cond_ref(x, itok_B_0_8, L2_cond_W1, L2_cond_b1, L2_cond_W2, L2_cond_b2, L2_cond_gamma, L2_cond_beta)
    x = x + _L3_cond_ref(x, L3_cond_s_init, condB_alphaparams, L3_cond_W1, L3_cond_b1, L3_cond_g1, L3_cond_be1, L3_cond_W2, L3_cond_b2, L3_cond_g2, L3_cond_be2, L3_cond_Wt, L3_cond_bt, L3_cond_gt, L3_cond_bet, 4)
    return x

_drawn_inputs = setup_inputs


def setup_inputs(seed=0):
    import zlib

    import numpy as np

    out = dict(_drawn_inputs(seed))
    spreads = {'L1_cond_ln_g': (1.0, 0.2),
     'L1_cond_ln_b': (0.0, 0.1),
     'L2_cond_b1': (0.0, 0.511),
     'L2_cond_b2': (0.0, 0.323),
     'L2_cond_gamma': (1.0, 0.2),
     'L2_cond_beta': (0.0, 0.1),
     'L3_cond_g1': (1.0, 0.2),
     'L3_cond_be1': (0.0, 0.294),
     'L3_cond_g2': (1.0, 0.2),
     'L3_cond_be2': (0.0, 0.269),
     'L3_cond_gt': (1.0, 0.2),
     'L3_cond_bet': (0.0, 0.1)}
    factors = {'L1_cond_down_b': 7.022,
     'L1_cond_up_b': 5.47,
     'L3_cond_b1': 8.0,
     'L3_cond_b2': 7.859,
     'L3_cond_bt': 3.176}
    for name, (base, spread) in spreads.items():
        noise = np.random.default_rng([zlib.crc32(name.encode()), seed]).standard_normal(out[name].shape)
        drawn = base * np.exp(spread * noise) if base else spread * noise
        out[name] = jnp.asarray(drawn.astype(out[name].dtype))
    for name, factor in factors.items():
        out[name] = (out[name] * factor).astype(out[name].dtype)
    return out
```

```python
from contextlib import ExitStack

import concourse.bass as bass
from concourse import mybir

ALU = mybir.AluOpType
ACT = mybir.ActivationFunctionType
F32 = mybir.dt.float32
F16 = mybir.dt.float16
I32 = mybir.dt.int32

P = 128
L = 16
D = 512
NT = D // P
BK = 128
F = 2048
FC = F // P
EVERY = 4
EPS = 1e-5
WS = 256.0

POST = {c: [("POST", c)] for c in range(NT)}
FRONT = {
    0: [("T", 0, 0)], 1: [("T", 0, 1)], 2: [("T", 0, 2)], 3: [("T", 0, 3), ("CW", 0), ("XB", 0, 0)],
    4: [("D", 0)],
    5: [("U", 0, 0), ("XB", 0, 1)],
    6: [("U", 0, 1), ("XB", 0, 2), ("T", 1, 0)],
    7: [("U", 0, 2), ("XB", 0, 3), ("T", 1, 1)],
    8: [("U", 0, 3), ("T", 1, 2)],
    9: [("T", 1, 3), ("CW", 1)],
    10: [("XB", 1, 0), ("D", 1)],
    11: [("U", 1, 0), ("XB", 1, 1)],
    12: [("U", 1, 1), ("XB", 1, 2)],
    13: [("U", 1, 2), ("XB", 1, 3)],
    14: [("U", 1, 3)],
    15: [("T", 2, 0), ("T", 2, 1), ("T", 2, 2), ("T", 2, 3)],
}
LZERO = {8: [("LP", 0)], 9: [("LP", 1), ("L0", 0)], 10: [("LP", 2), ("L0", 1)], 12: [("LP", 3)],
         15: [("L0", 2), ("L0", 3)]}
MIX = {
    1: [("CT", 0)], 2: [("CT", 1)], 3: [("CT", 2)], 4: [("CT", 3), ("WS", 0)],
    5: [("PC", 0), ("WS", 1)], 6: [("PC", 1), ("WS", 2)], 7: [("PC", 2), ("WS", 3)], 8: [("PC", 3)],
}
BACK = {11: [("GT", 0)], 12: [("GT", 1)], 13: [("GT", 2)], 14: [("GT", 3)],
        15: [("GO", 0), ("GO", 1), ("GO", 2), ("GO", 3)]}


def schedule(post, front, lzero, mix):
    parts = [POST] * post + [FRONT] * front + [LZERO] * lzero + [MIX] * (mix in "PQ") + [BACK] * (mix == "Q")
    return [[e for part in parts for e in part.get(c, [])] for c in range(FC)]


USES_F = ("T", "D", "U", "CT", "PC", "GT", "ST")


def f_banks(slots):
    uses = [e for slot in slots for e in slot if e[0] in USES_F] + [("ST",)]
    return {e: n % 2 for n, e in enumerate(uses)}


def build(nc, x, zx, zy, zr, id1, id2, alpha, dn_w1, dn_b1, up_w1, up_b1, ln_g1, ln_b1,
          dn_w2, dn_b2, up_w2, up_b2, ln_g2, ln_b2, s_init, w1, b1, g1, be1, w2, b2, g2, be2,
          wt, bt, gt, bet, out):
    dn_w, dn_b, up_w, up_b = (dn_w1, dn_w2), (dn_b1, dn_b2), (up_w1, up_w2), (up_b1, up_b2)
    ln_g, ln_b = (ln_g1, ln_g2), (ln_b1, ln_b2)
    n_ids = (7, 9)

    with ExitStack() as ctx:
        def sb(name, shape, dt=F32):
            return ctx.enter_context(nc.sbuf_tensor(name, shape, dt))

        def sem(name):
            return ctx.enter_context(nc.semaphore(name))

        ctx.enter_context(nc.allow_non_contiguous_dma(reason="bias columns and weights by chunk, small"))

        w1s = sb("w1s", [P, 2, NT, F], F16)
        w2s = sb("w2s", [P, 2, FC, D], F16)
        xr = sb("xr", [P, 2, NT, D])
        x1 = sb("x1", [P, NT, D])
        x3t = sb("x3t", [P, 2, NT, D], F16)
        ft = sb("ft", [P, 2, NT, D], F16)
        xin = sb("xin", [P, NT + 2, D])
        z = sb("z", [P, D])
        zs = sb("zs", [P, 2, D], F16)
        wraw = sb("wraw", [P, 2, D])
        ws = sb("ws", [P, 2, 2, D], F16)
        dnb = sb("dnb", [P, 1])
        vec = sb("vec", [P, 3, D])
        xb = sb("xb", [P, D])
        y = sb("y", [P, D])
        late = sb("late", [P, 4, NT, D])
        y4, pt, s, ctf = (late[:, n] for n in range(4))
        ct = ctf.rearrange("p a b -> p (a b)").bitcast(F16).rearrange("p (h k d) -> p h k d", h=2, k=NT)
        rows = sb("rows", [P, 5, D])
        crow, g2r, be2r, gtr, betr = (rows[:, n] for n in range(5))
        hs = sb("hs", [P, 2, 2, D], F16)
        sq = sb("sq", [P, D])
        hsum = sb("hsum", [P, 2, D])
        la = sb("la", [P, 2, D])
        lh = sb("lh", [P, 2, D])
        wtr = sb("wtr", [P, 2, NT, P])
        wts = sb("wts", [P, 2, NT, P], F16)
        ident = sb("ident", [P, P])
        ones = sb("ones", [P, 1])
        nhalf = sb("nhalf", [P, NT])
        eps = sb("eps", [P, 1])
        ids = sb("ids", [1, 2, L], I32)
        cin = sb("cin", [P, 4, L])
        coef = sb("coef", [P, L, 6])
        c0 = sb("c0", [P, 6])
        ca = sb("ca", [P, 6])
        b1c = sb("b1c", [P, FC])
        g1c = sb("g1c", [P, FC])
        be1c = sb("be1c", [P, FC])
        btc = sb("btc", [P, NT])
        mom = sb("mom", [P, NT, 2])
        msq = sb("msq", [P, NT])
        hvar = sb("hvar", [P, NT])
        rh = sb("rh", [P, NT])
        bn = sb("bn", [P, 6])
        mv = sb("mv", [P, 2])
        rs = sb("rs", [P, 1])
        bnp = sb("bnp", [P, 6])
        mvp = sb("mvp", [P, 2])
        rsp = sb("rsp", [P, 1])
        bng = sb("bng", [P, 6])
        mvg = sb("mvg", [P, 2])
        rsg = sb("rsg", [P, 1])

        phi = ctx.enter_context(nc.psum_tensor("phi", [P, NT, D], F32))
        hp = ctx.enter_context(nc.psum_tensor("hp", [P, 2, D], F32))
        fp = ctx.enter_context(nc.psum_tensor("fp", [P, 2, D], F32))

        s_small = sem("s_small")
        s_ids = sem("s_ids")
        s_cst = sem("s_cst")
        s_coef = sem("s_coef")
        s_sig = sem("s_sig")
        s_step = sem("s_step")
        s_w1ld = [sem(f"s_w1ld{k}") for k in range(NT)]
        s_w2ld = [sem(f"s_w2ld{k}") for k in range(NT)]
        s_wsh, s_wsl = sem("s_wsh"), sem("s_wsl")
        s_csum = sem("s_csum")
        s_cs = sem("s_cs")
        s_cen = sem("s_cen")
        s_sld = sem("s_sld")
        w1_done, gelu_done, hi_done, sq_done = sem("w1_done"), sem("gelu_done"), sem("hi_done"), sem("sq_done")
        lo_done, sum_done, sumsq_done, w2_done = sem("lo_done"), sem("sum_done"), sem("sumsq_done"), sem("w2_done")
        phi_done = sem("phi_done")
        stats_done = sem("stats_done")
        ca_done, mom_done, rh_done = sem("ca_done"), sem("mom_done"), sem("rh_done")
        y2_done, bnp_done, mvp_done, s1_done = sem("y2_done"), sem("bnp_done"), sem("mvp_done"), sem("s1_done")
        s2_done, tp_done, rsp_done, s_done = sem("s2_done"), sem("tp_done"), sem("rsp_done"), sem("s_done")
        out_done = sem("out_done")
        st_done = sem("st_done")
        xin_ld = sem("xin_ld")
        raw_ld, vec_ld = sem("raw_ld"), sem("vec_ld")
        wc_hi, wc_lo = sem("wc_hi"), sem("wc_lo")
        tr_done, thi_done, tlo_done = sem("tr_done"), sem("thi_done"), sem("tlo_done")
        dn_done, relu_done, zhi_done, zlo_done = sem("dn_done"), sem("relu_done"), sem("zhi_done"), sem("zlo_done")
        up_done, yf_done, bnf_done, mvf_done = sem("up_done"), sem("yf_done"), sem("bnf_done"), sem("mvf_done")
        tf_done, rsf_done, xn_done = sem("tf_done"), sem("rsf_done"), sem("xn_done")
        xb_done, xg_done = sem("xb_done"), sem("xg_done")
        c0_done = sem("c0_done")
        l0v, l0h, l0a, l0q, l0s, l0x = (sem(n) for n in ("l0v", "l0h", "l0a", "l0q", "l0s", "l0x"))
        ctr_done, chi_done, clo_done = sem("ctr_done"), sem("chi_done"), sem("clo_done")
        wt_ld = [sem("wt_ld0"), sem("wt_ld1")]
        wth_done, wtl_done, pc_done = sem("wth_done"), sem("wtl_done"), sem("pc_done")
        pe_done = sem("pe_done")
        qa_done, qg_done = sem("qa_done"), sem("qg_done")
        xs_done = sem("xs_done")
        gt_done, gbn_done, gmv_done, gy_done = sem("gt_done"), sem("gbn_done"), sem("gmv_done"), sem("gy_done")
        grs_done, gs_done, go_done, sc_done = sem("grs_done"), sem("gs_done"), sem("go_done"), sem("sc_done")
        gst_done = sem("gst_done")

        def wait(eng, s_, value):
            if isinstance(value, int) and value <= 0:
                return
            eng.wait_ge(s_, value)

        def wait_split_free(eng, l, c):
            if c == 1:
                wait(eng, phi_done, l * NT)
            else:
                wait(eng, w2_done, l * (FC - 1) + max(c - 1, 0))

        def rows_of(ap):
            return ap.rearrange("(p r) d -> p r d", r=NT)

        class It:

            def __init__(self, g, j, post=True, front=True, lzero=True, mix="-"):
                self.g, self.j = g, j
                self.l = g * EVERY + j
                self.post, self.front, self.lzero, self.mix = post, front, lzero, mix
                self.m = self.l + 1
                self.par = (j + 1) % 2
                self.slots = schedule(post, front, lzero, mix)
                self.bank = f_banks(self.slots)
                self.cg = g if mix == "P" else g - 1 if j == 0 else g
                self.k = self.cg * 2 + (mix == "Q")

        def stored(g, j):
            return g * (EVERY - 1) + j

        def iterations(eng, body):
            body(It(0, 0, post=False))
            body(It(0, 1))
            body(It(0, 2, mix="P"))
            body(It(0, 3))
            body(It(0, 4, mix="Q"))
            with eng.Fori(1, L // EVERY - 1) as g:
                body(It(g, 1))
                body(It(g, 2, mix="P"))
                body(It(g, 3))
                body(It(g, 4, mix="Q"))
            body(It(L // EVERY - 1, 1))
            body(It(L // EVERY - 1, 2, lzero=False, mix="P"))
            body(It(L // EVERY - 1, 3, front=False, lzero=False))

        PRE = [e for c in range(FC) for e in FRONT[c]]
        PRE_BANK = f_banks([PRE])
        LAST = It(L // EVERY - 1, 4, front=False, lzero=False, mix="Q")
        LAST_EVENTS = [("CT", 0), ("CT", 1), ("CT", 2), ("CT", 3), ("WS", 0), ("PC", 0), ("WS", 1), ("PC", 1),
                       ("WS", 2), ("PC", 2), ("WS", 3), ("PC", 3), ("GT", 0), ("GT", 1), ("GT", 2), ("GT", 3),
                       ("GO", 0), ("GO", 1), ("GO", 2), ("GO", 3)]
        LAST.bank = f_banks([LAST_EVENTS])

        block = ctx.enter_context(nc.Block())

        @block.sync
        def _(sp):
            def load_x(m, free):
                if free is not None:
                    wait(sp, l0x, free)
                src = x[m] if isinstance(m, int) else x[bass.ds(m, 1)].rearrange("a r d -> (a r) d")
                for dst, rws in ((xin[:, 1:NT + 1], rows_of(src)),
                                 (xin[1:P - 1, 0], src[3:D - 8:NT]), (xin[P - 1:P, 0], src[D - 5:D - 4]),
                                 (xin[0:1, 0], src[1:2]),
                                 (xin[0:P - 2, NT + 1], src[NT:D - 4:NT]), (xin[P - 2:P - 1, NT + 1], src[D - 4:D - 3]),
                                 (xin[P - 1:P, NT + 1], src[D - 2:D - 1])):
                    sp.dma_start(dst, rws).then_inc(xin_ld, 16)

            def pick(y_, m):
                i = ids[0:1, y_, m:m + 1] if isinstance(m, int) else ids[0:1, y_, bass.ds(m, 1)]
                return sp.value_load(i, min_val=0, max_val=n_ids[y_] - 1)

            def load_raw(m, y_):
                i = pick(y_, m)
                wait(sp, wc_lo, m * 2 + y_)
                sp.dma_start(wraw[:, 0].rearrange("p (k b) -> p k b", k=NT),
                             dn_w[y_][bass.ds(i, 1)].rearrange("a (k p) b -> p (a k) b", p=P)).then_inc(raw_ld, 16)
                sp.dma_start(wraw[:, 1], up_w[y_][bass.ds(i, 1)].rearrange("a k d -> (a k) d")).then_inc(raw_ld, 16)

            def load_vec(m, y_):
                i = pick(y_, m)
                wait(sp, xn_done, (m * 2 + y_) * NT)
                for n, t in enumerate((up_b[y_], ln_g[y_], ln_b[y_])):
                    sp.dma_start(vec[:, n], t[bass.ds(i, 1)].to_broadcast([P, D])).then_inc(vec_ld, 16)
                sp.dma_start(dnb[:, :], dn_b[y_][bass.ds(i, 1)].rearrange("a p -> p a")).then_inc(vec_ld, 16)

            for n, t in enumerate((id1, id2)):
                sp.dma_start(ids[:, n], t.rearrange("(a n) -> a n", a=1)).then_inc(s_ids, 16)
            load_x(0, None)
            for n, t in enumerate((zx, zy, zr, alpha)):
                sp.dma_start(cin[:, n], t.rearrange("(a n) -> a n", a=1).to_broadcast([P, L])).then_inc(s_small, 16)
            sp.dma_start(b1c[:, :], b1.rearrange("(c p) -> p c", p=P)).then_inc(s_small, 16)
            sp.dma_start(g1c[:, :], g1.rearrange("(c p) -> p c", p=P)).then_inc(s_small, 16)
            sp.dma_start(be1c[:, :], be1.rearrange("(c p) -> p c", p=P)).then_inc(s_small, 16)
            sp.dma_start(btc[:, :], bt.rearrange("(c p) -> p c", p=P)).then_inc(s_small, 16)
            for n, t in enumerate((b2, g2, be2, gt, bet)):
                sp.dma_start(rows[:, n], t.rearrange("(a n) -> a n", a=1).to_broadcast([P, D])).then_inc(s_small, 16)
            sp.wait_ge(s_ids, 32)
            load_raw(0, 0)
            load_vec(0, 0)
            for k in range(NT):
                sp.dma_start(late[:, k].rearrange("p a b -> p (a b)"), w1[k * P:(k + 1) * P, :]).then_inc(s_w1ld[k], 16)
            load_raw(0, 1)
            load_vec(0, 1)
            for k in range(NT):
                sp.wait_ge(s_wsl, k + 1)
                sp.dma_start(late[:, k], w2.rearrange("(q c p) d -> q p c d", p=P, q=NT)[k]).then_inc(s_w2ld[k], 16)
            load_raw(1, 0)
            load_x(1, NT)
            sp.wait_ge(s_wsl, NT + FC)
            sp.dma_start(s, rows_of(s_init)).then_inc(s_sld, 16)

            def body(it):
                if it.lzero:
                    load_x(it.m + 1, (it.m + 1) * NT)
                if it.front:
                    load_vec(it.m, 0)
                    load_raw(it.m, 1)
                n, jl = stored(it.g, it.j - 1), it.j - 1
                if it.post and jl % EVERY != EVERY - 1:
                    store(n, it.l - 1, jl % 2)
                if it.front:
                    load_vec(it.m, 1)
                if it.lzero:
                    load_raw(it.m + 1, 0)
                if it.mix == "Q":
                    store_ck(it)

            def store(n, l, par):
                dst = out[l] if isinstance(l, int) else out[bass.ds(l, 1)].rearrange("a r d -> (a r) d")
                for j in range(NT):
                    wait(sp, out_done, n * NT + j + 1)
                    sp.dma_start(rows_of(dst)[:, j], xr[:, par, j]).then_inc(st_done, 16)

            def store_ck(it):
                l = it.l - 1
                dst = out[l] if isinstance(l, int) else out[bass.ds(l, 1)].rearrange("a r d -> (a r) d")
                for j in range(NT):
                    wait(sp, go_done, it.cg * NT + j + 1)
                    sp.dma_start(rows_of(dst)[:, j], pt[:, j]).then_inc(gst_done, 16)

            iterations(sp, body)
            store_ck(LAST)
            sp.wait_ge(st_done, 64 * (L - L // EVERY))
            sp.wait_ge(gst_done, 64 * (L // EVERY))

        @block.gpsimd
        def _(pool):
            def tt(out_, a, b, op, done):
                pool.tensor_tensor(out_, a, b, op).then_inc(done, 1)

            def rstd(dst, src, n, done, add_done=None):
                tt(dst, src, eps[:, :], ALU.add, done)
                wait(pool, done, n + 1)
                tt(dst, dst, nhalf[:, 0:1], ALU.pow, done)

            def event(e, it):
                m = it.m
                if e[0] == "XB":
                    y_, j = e[1:]
                    i = m * 8 + 4 * y_ + j
                    src = x1[:, j] if y_ == 0 else xr[:, it.par, j]
                    if y_ == 0:
                        wait(pool, l0x, m * NT + j + 1)
                    else:
                        wait(pool, xn_done, m * 8 + j + 1)
                        wait(pool, tr_done, m * 12 + NT + j + 1)
                    wait(pool, vec_ld, (m * 2 + y_ + 1) * 64)
                    wait(pool, yf_done, i)
                    tt(xb[:, :], src, vec[:, 0], ALU.add, xb_done)
                    if y_ == 0:
                        free_xr(it)
                    tt(xr[:, it.par, j], src, vec[:, 2], ALU.add, xg_done)
                if e[0] == "U":
                    y_, j = e[1:]
                    i = m * 8 + 4 * y_ + j
                    wait(pool, mvf_done, i + 1)
                    rstd(rs[:, :], mv[:, 1:2], i * 2, rsf_done)
                if e[0] == "POST":
                    l, j = it.l - 1, e[1]
                    i = l * NT + j
                    wait(pool, mvp_done, i + 1)
                    rstd(rsp[:, :], mvp[:, 1:2], i * 3, rsp_done)
                    wait(pool, rsp_done, i * 3 + 2)
                    tt(rsp[:, :], rsp[:, :], ca[:, 4:5], ALU.mult, rsp_done)
                    if it.j % EVERY != 0:
                        wait(pool, s_done, i + 1)
                        r = xr[:, (it.j - 1) % 2, j]
                        tt(r, r, s[:, j], ALU.add, out_done)
                if e[0] == "LP":
                    lap(m + 1, e[1])
                if e[0] == "GT":
                    i = it.cg * NT + e[1]
                    wait(pool, gmv_done, i + 1)
                    rstd(rsg[:, :], mvg[:, 1:2], i * 2, grs_done)
                if e[0] == "GO":
                    i = it.cg * NT + e[1]
                    wait(pool, gs_done, i + 1)
                    wait(pool, xs_done, i + 1)
                    wait(pool, gt_done, (it.cg + 1) * NT)
                    tt(pt[:, e[1]], y4[:, e[1]], s[:, e[1]], ALU.add, go_done)

            def free_xr(it):
                jp = it.j - 1
                if jp < 0:
                    return
                if jp % EVERY != EVERY - 1:
                    wait(pool, st_done, (stored(it.g, jp) + 1) * 64)
                else:
                    wait(pool, xs_done, (it.cg + 1) * NT)

            def lap(m, r):
                i, b = m * NT + r, r % 2
                if r == 0:
                    wait(pool, xin_ld, (m + 1) * 112)
                wait(pool, tlo_done, 12 * (m - 1) + r + 1)
                wait(pool, xg_done, 8 * (m - 1) + r + 1)
                tt(x1[:, r], xin[:, r], xin[:, r + 2], ALU.add, l0v)
                wait(pool, l0x, i - 1)
                c = xin[:, r + 1]
                tt(lh[:, b, 1:D - 1], c[:, 0:D - 2], c[:, 2:D], ALU.add, l0h)
                tt(lh[:, b, 0:D:D - 1], c[:, 1:D - 1:D - 3], c[:, 1:D - 1:D - 3], ALU.add, l0h)
                wait(pool, l0a, i + 1)
                tt(la[:, b], la[:, b], c, ALU.mult, l0q)

            pool.memset(ident[:, :], 0.0).then_inc(s_cst, 1)
            pool.memset(ones[:, :], 1.0).then_inc(s_cst, 1)
            pool.memset(nhalf[:, :], -0.5).then_inc(s_cst, 1)
            pool.memset(eps[:, :], EPS).then_inc(s_cst, 1)
            pool.wait_ge(s_cst, 4)
            pool.affine_select(out=ident[:, :], in_=ident[:, :], compare_op=ALU.not_equal, fill=1.0, base=0,
                               pattern=[[-1, P]], channel_multiplier=1).then_inc(s_cst, 1)
            for r in range(NT):
                lap(0, r)
            pre = It(0, -1, post=False)
            for e in PRE:
                event(e, pre)
            for r in range(NT):
                lap(1, r)

            def rh_step(l):
                wait(pool, mom_done, l * 4 + 4)
                tt(rh[:, :], hvar[:, :], nhalf[:, :], ALU.pow, rh_done)

            def body(it):
                if it.post:
                    rh_step(it.l - 1)
                for c in range(FC):
                    for e in it.slots[c]:
                        event(e, it)

            iterations(pool, body)
            rh_step(L - 1)
            for j in range(NT):
                event(("POST", j), LAST)
            for e in LAST_EVENTS:
                event(e, LAST)

        @block.scalar
        def _(act):
            def copy(out_, in_, done, scale=1.0):
                act.activation(out_, in_, ACT.Copy, scale=scale).then_inc(done, 1)

            def gelu_step(n, c):
                wait(act, w1_done, n + 1)
                act.activation(hp[:, c % 2], hp[:, c % 2], ACT.Gelu, bias=b1c[:, c:c + 1],
                               scale=1.0 / WS).then_inc(gelu_done, 1)

            def hi_step(l, n, c):
                wait(act, gelu_done, n + 1)
                wait_split_free(act, l, c)
                copy(hs[:, c % 2, 0], hp[:, c % 2], hi_done)
                wait(act, sumsq_done, n)
                act.activation(sq[:, :], hp[:, c % 2], ACT.Square).then_inc(sq_done, 1)

            def event(e, it):
                m, bank = it.m, it.bank.get(e)
                if e[0] == "T":
                    t, j = e[1:]
                    i = m * 12 + 4 * t + j
                    wait(act, tr_done, i + 1)
                    dst = x3t if t == 2 else ft
                    if t == 2:
                        wait(act, w1_done, m * FC)
                    else:
                        wait(act, dn_done, m * 2 + t)
                    copy(dst[:, 0, :, j * P:(j + 1) * P], fp[:, bank].rearrange("p (k q) -> p k q", k=NT), thi_done)
                if e[0] == "CW":
                    w = m * 2 + e[1]
                    wait(act, raw_ld, (w + 1) * 32)
                    wait(act, up_done, w * NT)
                    copy(ws[:, 0], wraw[:, :], wc_hi, scale=WS)
                if e[0] == "D":
                    w = m * 2 + e[1]
                    wait(act, dn_done, w + 1)
                    wait(act, vec_ld, (w + 1) * 64)
                    wait(act, zlo_done, w)
                    act.activation(z[:, :], fp[:, bank], ACT.Relu, bias=dnb[:, 0:1], scale=1.0 / WS)\
                       .then_inc(relu_done, 1)
                    wait(act, relu_done, w + 1)
                    wait(act, up_done, w * NT)
                    copy(zs[:, 0], z[:, :], zhi_done)
                if e[0] == "POST":
                    l, j = it.l - 1, e[1]
                    i = l * NT + j
                    wait(act, ca_done, l + 1)
                    s_before(it, l, j)
                    act.activation(s[:, j], s[:, j], ACT.Copy, scale=ca[:, 5:6]).then_inc(s1_done, 1)
                if e[0] == "LP":
                    lap(m + 1, e[1])
                if e[0] == "CT":
                    i = it.k * NT + e[1]
                    wait(act, ctr_done, i + 1)
                    wait(act, pc_done, it.k * NT)
                    copy(ct[:, 0, :, e[1] * P:(e[1] + 1) * P], fp[:, bank].rearrange("p (k q) -> p k q", k=NT), chi_done)
                    if it.mix == "Q":
                        copy(s[:, e[1]], xr[:, 1, e[1]], xs_done)
                    if e[1] == NT - 2:
                        load_wt(it, 0)
                        load_wt(it, 1)
                if e[0] == "WS":
                    n = it.k * NT + e[1]
                    wait(act, wt_ld[e[1] % 2], (it.k * 2 + e[1] // 2 + 1) * 16)
                    wait(act, pc_done, n)
                    copy(wts[:, 0], wtr[:, e[1] % 2], wth_done, scale=WS)
                if e[0] == "PC":
                    n = it.k * NT + e[1]
                    if e[1] + 2 < NT:
                        load_wt(it, e[1] + 2)
                    if it.mix == "P":
                        wait(act, pc_done, n + 1)
                        wait(act, gst_done, it.cg * 64)
                        copy(pt[:, e[1]], fp[:, bank], pe_done, scale=1.0 / WS)
                    else:
                        i = it.cg * NT + e[1]
                        wait(act, qa_done, i + 1)
                        act.activation(pt[:, e[1]], pt[:, e[1]], ACT.Gelu, bias=btc[:, e[1]:e[1] + 1])\
                           .then_inc(qg_done, 1)
                if e[0] == "GO":
                    i = it.cg * NT + e[1]
                    wait(act, go_done, i + 1)
                    copy(s[:, e[1]], y4[:, e[1]], sc_done)

            def load_wt(it, mm):
                n = it.k * NT + mm
                half = D if it.mix == "P" else 0
                wait(act, wtl_done, n - 1)
                act.dma_start(wtr[:, mm % 2], wt[half:half + D, mm * P:(mm + 1) * P]
                              .rearrange("(k p) n -> p k n", p=P)).then_inc(wt_ld[mm % 2], 16)

            def s_before(it, l, j):
                prev = (it.j - 2) % EVERY
                if isinstance(it.l, int) and it.l == 1:
                    wait(act, s_sld, 16)
                    return
                if prev == EVERY - 1:
                    q = it.g if it.j == 1 else it.g + 1
                    if j == 0:
                        wait(act, sc_done, q * NT)
                else:
                    n = stored(it.g, it.j - 2)
                    wait(act, s_done, l * NT - NT + j + 1)
                    wait(act, out_done, n * NT + j + 1)
                    if prev == 1:
                        wait(act, ctr_done, it.g * 8 + j + 1)

            def lap(n, r):
                i = n * NT + r
                wait(act, c0_done, n + 1)
                wait(act, xin_ld, (n + 1) * 112)
                wait(act, l0x, i - 1)
                act.activation(la[:, r % 2], xin[:, r + 1], ACT.Identity, bias=c0[:, 0:1], scale=c0[:, 1:2])\
                   .then_inc(l0a, 1)

            act.wait_ge(s_small, 13 * 16)
            act.wait_ge(s_coef, 4)
            act.activation(coef[:, :, 4], cin[:, 3], ACT.Sigmoid).then_inc(s_sig, 1)
            for r in range(NT):
                lap(0, r)
            for k in range(NT):
                act.wait_ge(s_w1ld[k], 16)
                copy(w1s[:, 0, k], late[:, k].rearrange("p a b -> p (a b)"), s_wsh, scale=WS)
            pre = It(0, -1, post=False)
            for e in PRE:
                event(e, pre)
            for c in range(FC):
                act.wait_ge(s_cen, c + 1)
                copy(w2s[:, 0, c], late[:, c // NT, c % NT], s_wsh, scale=WS)
            for r in range(NT):
                lap(1, r)

            def body(it):
                n = it.l * FC
                gelu_step(n, 0)
                hi_step(it.l, n, 0)
                for c in range(FC):
                    if c + 1 < FC:
                        gelu_step(n + c + 1, c + 1)
                    for e in it.slots[c]:
                        event(e, it)
                    if c + 1 < FC:
                        hi_step(it.l, n + c + 1, c + 1)

            iterations(act, body)
            for j in range(NT):
                event(("POST", j), LAST)
            for e in LAST_EVENTS:
                event(e, LAST)

        @block.vector
        def _(dve):
            def stt(out_, a, sc, b, op0, op1, done):
                dve.scalar_tensor_tensor(out_, a, sc, b, op0, op1).then_inc(done, 1)

            def aggr(out_, in_, bn_sem, n, done):
                wait(dve, bn_sem, n)
                dve.sem_inc(s_step)
                dve.bn_aggr(out_, in_).then_inc(done, 1)

            def chunk(it, c):
                l, n, b = it.l, it.l * FC + c, c % 2
                wait(dve, hi_done, n + 1)
                wait(dve, sq_done, n + 1)
                wait_split_free(dve, l, c)
                stt(hs[:, b, 1], hp[:, b], 1.0, hs[:, b, 0], ALU.mult, ALU.subtract, lo_done)
                if c == 0:
                    wait(dve, stats_done, l)
                    dve.tensor_copy(hsum[:, 0], hp[:, b]).then_inc(sum_done, 1)
                    dve.tensor_copy(hsum[:, 1], sq[:, :]).then_inc(sumsq_done, 1)
                else:
                    wait(dve, sum_done, n)
                    dve.tensor_tensor(hsum[:, 0], hp[:, b], hsum[:, 0], ALU.add).then_inc(sum_done, 1)
                    wait(dve, sumsq_done, n)
                    dve.tensor_tensor(hsum[:, 1], hsum[:, 1], sq[:, :], ALU.add).then_inc(sumsq_done, 1)

            def moments(it, l, bank):
                st = fp[:, bank, 0:2 * NT].rearrange("p (j w) -> p j w", w=2)
                wait(dve, rsp_done, l * NT * 3)
                wait(dve, s2_done, l * NT)
                row = coef[:, l] if isinstance(l, int) else coef[:, bass.ds(l, 1)].rearrange("p a n -> p (a n)")
                dve.sem_inc(s_step)
                dve.tensor_copy(ca[:, :], row).then_inc(ca_done, 1)
                wait(dve, stats_done, l + 1)
                wait(dve, y2_done, l * NT)
                i = l * 4
                dve.tensor_scalar(mom[:, :, 0], st[:, :, 0], WS / F, None, ALU.mult).then_inc(mom_done, 1)
                dve.tensor_scalar(mom[:, :, 1], st[:, :, 1], WS * WS / F, WS * WS * EPS, ALU.mult, ALU.add)\
                   .then_inc(mom_done, 1)
                wait(dve, mom_done, i + 2)
                dve.tensor_tensor(msq[:, :], mom[:, :, 0], mom[:, :, 0], ALU.mult).then_inc(mom_done, 1)
                wait(dve, mom_done, i + 3)
                wait(dve, rh_done, l)
                dve.tensor_tensor(hvar[:, :], mom[:, :, 1], msq[:, :], ALU.subtract).then_inc(mom_done, 1)
                wait(dve, rh_done, l + 1)
                for j in range(NT):
                    n = l * NT + j
                    wait(dve, phi_done, n + 1)
                    y4_free(it, l, j)
                    stt(y4[:, j], phi[:, j], rh[:, j:j + 1], crow, ALU.mult, ALU.add, y2_done)

            def y4_free(it, l, j):
                if isinstance(it.l, int) and it.l == 1:
                    return
                wait(dve, s_done, (l - 1) * NT + j + 1)
                if (it.j - 2) % EVERY == EVERY - 1:
                    q = it.g if it.j == 1 else it.g + 1
                    wait(dve, sc_done, q * NT)

            def event(e, it):
                m, bank = it.m, it.bank.get(e)
                if e[0] == "T":
                    t, j = e[1:]
                    i = m * 12 + 4 * t + j
                    wait(dve, thi_done, i + 1)
                    dst = x3t if t == 2 else ft
                    cols = slice(j * P, (j + 1) * P)
                    stt(dst[:, 1, :, cols], fp[:, bank].rearrange("p (k q) -> p k q", k=NT), 1.0, dst[:, 0, :, cols],
                        ALU.mult, ALU.subtract, tlo_done)
                if e[0] == "CW":
                    w = m * 2 + e[1]
                    wait(dve, wc_hi, w + 1)
                    stt(ws[:, 1], wraw[:, :], WS, ws[:, 0], ALU.mult, ALU.subtract, wc_lo)
                if e[0] == "D":
                    w = m * 2 + e[1]
                    wait(dve, zhi_done, w + 1)
                    stt(zs[:, 1], z[:, :], 1.0, zs[:, 0], ALU.mult, ALU.subtract, zlo_done)
                if e[0] == "U":
                    y_, j = e[1:]
                    i = m * 8 + 4 * y_ + j
                    wait(dve, up_done, i + 1)
                    wait(dve, xb_done, i + 1)
                    wait(dve, xn_done, i)
                    stt(y[:, :], fp[:, bank], 1.0 / WS, xb[:, :], ALU.mult, ALU.add, yf_done)
                    wait(dve, yf_done, i + 1)
                    dve.bn_stats(bn[:, :], y[:, :]).then_inc(bnf_done, 1)
                    wait(dve, rsf_done, i * 2)
                    aggr(mv[:, :], bn[:, :], bnf_done, i + 1, mvf_done)
                    wait(dve, mvf_done, i + 1)
                    stt(y[:, :], y[:, :], mv[:, 0:1], vec[:, 1], ALU.subtract, ALU.mult, tf_done)
                    wait(dve, tf_done, i + 1)
                    wait(dve, rsf_done, i * 2 + 2)
                    wait(dve, xg_done, i + 1)
                    r = xr[:, it.par, j]
                    stt(r, y[:, :], rs[:, 0:1], r, ALU.mult, ALU.add, xn_done)
                if e[0] == "POST":
                    l, j = it.l - 1, e[1]
                    i = l * NT + j
                    wait(dve, y2_done, i + 1)
                    dve.bn_stats(bnp[:, :], y4[:, j]).then_inc(bnp_done, 1)
                    wait(dve, rsp_done, i * 3)
                    aggr(mvp[:, :], bnp[:, :], bnp_done, i + 1, mvp_done)
                    wait(dve, s1_done, i + 1)
                    stt(s[:, j], be2r, ca[:, 4:5], s[:, j], ALU.mult, ALU.add, s2_done)
                    wait(dve, mvp_done, i + 1)
                    stt(y4[:, j], y4[:, j], mvp[:, 0:1], g2r, ALU.subtract, ALU.mult, tp_done)
                    wait(dve, tp_done, i + 1)
                    wait(dve, s2_done, i + 1)
                    wait(dve, rsp_done, i * 3 + 3)
                    stt(s[:, j], y4[:, j], rsp[:, 0:1], s[:, j], ALU.mult, ALU.add, s_done)
                if e[0] == "L0":
                    lap(m + 1, e[1])
                if e[0] == "CT":
                    i = it.k * NT + e[1]
                    cols = slice(e[1] * P, (e[1] + 1) * P)
                    wait(dve, chi_done, i + 1)
                    stt(ct[:, 1, :, cols], fp[:, bank].rearrange("p (k q) -> p k q", k=NT), 1.0, ct[:, 0, :, cols],
                        ALU.mult, ALU.subtract, clo_done)
                if e[0] == "WS":
                    n = it.k * NT + e[1]
                    wait(dve, wth_done, n + 1)
                    stt(wts[:, 1], wtr[:, e[1] % 2], WS, wts[:, 0], ALU.mult, ALU.subtract, wtl_done)
                if e[0] == "PC" and it.mix == "Q":
                    i = it.cg * NT + e[1]
                    wait(dve, pc_done, it.k * NT + e[1] + 1)
                    wait(dve, pe_done, i + 1)
                    stt(pt[:, e[1]], fp[:, bank], 1.0 / WS, pt[:, e[1]], ALU.mult, ALU.add, qa_done)
                if e[0] == "GT":
                    j = e[1]
                    i = it.cg * NT + j
                    wait(dve, gt_done, i + 1)
                    dve.bn_stats(bng[:, :], fp[:, bank]).then_inc(gbn_done, 1)
                    wait(dve, grs_done, i * 2)
                    aggr(mvg[:, :], bng[:, :], gbn_done, i + 1, gmv_done)
                    wait(dve, gmv_done, i + 1)
                    wait(dve, s_done, (it.l - 1) * NT + j + 1)
                    stt(y4[:, j], fp[:, bank], mvg[:, 0:1], gtr, ALU.subtract, ALU.mult, gy_done)
                    wait(dve, gy_done, i + 1)
                    wait(dve, grs_done, i * 2 + 2)
                    stt(y4[:, j], y4[:, j], rsg[:, 0:1], betr, ALU.mult, ALU.add, gs_done)

            def lap(n, r):
                i = n * NT + r
                wait(dve, l0q, i + 1)
                a, b = la[:, r % 2], lh[:, r % 2]
                stt(a, x1[:, r], c0[:, 3:4], a, ALU.mult, ALU.add, l0s)
                wait(dve, l0s, i + 1)
                stt(x1[:, r], b, c0[:, 2:3], a, ALU.mult, ALU.add, l0x)

            def pick_c0(n):
                wait(dve, l0x, n * NT)
                dve.sem_inc(s_step)
                row = coef[:, n] if isinstance(n, int) else coef[:, bass.ds(n, 1)].rearrange("p a n -> p (a n)")
                dve.tensor_copy(c0[:, :], row).then_inc(c0_done, 1)

            dve.wait_ge(s_small, 13 * 16)
            dve.tensor_tensor(coef[:, :, 0], cin[:, 0], cin[:, 1], ALU.add).then_inc(s_coef, 1)
            dve.tensor_scalar(coef[:, :, 1], cin[:, 2], -1.0, None, ALU.mult).then_inc(s_coef, 1)
            dve.tensor_copy(coef[:, :, 2], cin[:, 0]).then_inc(s_coef, 1)
            dve.tensor_copy(coef[:, :, 3], cin[:, 1]).then_inc(s_coef, 1)
            dve.wait_ge(s_coef, 4)
            dve.tensor_scalar(coef[:, :, 0], coef[:, :, 0], -2.0, 1.0, ALU.mult, ALU.add).then_inc(s_coef, 1)
            dve.wait_ge(s_coef, 5)
            dve.tensor_tensor(coef[:, :, 0], coef[:, :, 0], cin[:, 2], ALU.add).then_inc(s_coef, 1)
            dve.wait_ge(s_sig, 1)
            dve.tensor_scalar(coef[:, :, 5], coef[:, :, 4], -1.0, 1.0, ALU.mult, ALU.add).then_inc(s_coef, 1)
            dve.wait_ge(s_coef, 7)
            pick_c0(0)
            for r in range(NT):
                lap(0, r)
            for k in range(NT):
                dve.wait_ge(s_wsh, k + 1)
                stt(w1s[:, 1, k], late[:, k].rearrange("p a b -> p (a b)"), WS, w1s[:, 0, k], ALU.mult, ALU.subtract,
                    s_wsl)
            pre = It(0, -1, post=False)
            for e in PRE:
                event(e, pre)
            dve.wait_ge(s_csum, 1)
            dve.tensor_tensor(crow, phi[:, 0], crow, ALU.add).then_inc(s_cs, 1)
            wait(dve, xn_done, 8)
            dve.tensor_scalar(y[:, :], phi[:, 1], 1.0 / F, None, ALU.mult).then_inc(s_cs, 1)
            dve.wait_ge(s_cs, 2)
            for c in range(FC):
                w = late[:, c // NT, c % NT]
                stt(w, w, g1c[:, c:c + 1], y[:, :], ALU.mult, ALU.subtract, s_cen)
            for c in range(FC):
                dve.wait_ge(s_wsh, NT + c + 1)
                stt(w2s[:, 1, c], late[:, c // NT, c % NT], WS, w2s[:, 0, c], ALU.mult, ALU.subtract, s_wsl)
            pick_c0(1)
            for r in range(NT):
                lap(1, r)

            def body(it):
                if it.post:
                    moments(it, it.l - 1, bank=0)
                if it.lzero:
                    pick_c0(it.m + 1)
                chunk(it, 0)
                for c in range(FC):
                    for e in it.slots[c]:
                        event(e, it)
                    if c + 1 < FC:
                        chunk(it, c + 1)

            iterations(dve, body)
            moments(LAST, L - 1, bank=0)
            for j in range(NT):
                event(("POST", j), LAST)
            for e in LAST_EVENTS:
                event(e, LAST)

        @block.tensor
        def _(pe):
            release = {}

            def take(it, e, who, count):
                b = it.bank[e]
                if b in release:
                    wait(pe, *release[b])
                release[b] = (who, count)
                return fp[:, b]

            def mm3(out_, lhs, rhs, pairs, done=None):
                n = len(pairs)
                for q, (a, b) in enumerate(pairs):
                    for t, (u, v) in enumerate(((0, 0), (0, 1), (1, 0))):
                        last = pe.matmul(out_, lhs(u, a), rhs(v, b), start=(q == 0 and t == 0),
                                         stop=(q == n - 1 and t == 2))
                if done is not None:
                    last.then_inc(done, 1)

            def turn(bank, src, done):
                for k in range(NT):
                    last = pe.transpose(bank[:, k * P:(k + 1) * P], src(k), ident[:, :])
                last.then_inc(done, 1)

            ks = [(k, k) for k in range(NT)]

            def up_chunk(l, c):
                n = l * FC + c
                if c == 0:
                    wait(pe, tlo_done, l * 12 + 12)
                wait(pe, sum_done, n - 1)
                mm3(hp[:, c % 2], lambda u, k: w1s[:, u, k, c * P:(c + 1) * P], lambda v, k: x3t[:, v, k], ks, w1_done)

            def down_tile(it, c, j):
                n = it.l * FC + c
                if j == 0:
                    wait(pe, lo_done, n + 1)
                if c == 0 and it.post:
                    wait(pe, y2_done, (it.l - 1) * NT + j + 1)
                for t, (u, v) in enumerate(((0, 0), (0, 1), (1, 0))):
                    last = pe.matmul(phi[:, j], hs[:, c % 2, u, j * P:(j + 1) * P], w2s[:, v, c],
                                     start=(c == 0 and t == 0), stop=(c == FC - 1 and t == 2))
                if c == FC - 1:
                    last.then_inc(phi_done, 1)
                elif j == NT - 1:
                    last.then_inc(w2_done, 1)

            def event(e, it):
                m = it.m
                if e[0] == "T":
                    t, j = e[1:]
                    i = m * 12 + 4 * t + j
                    if t == 0:
                        wait(pe, l0x, m * NT + j + 1)
                    else:
                        wait(pe, xn_done, m * 8 + NT * (t - 1) + j + 1)
                    src = x1[:, j] if t == 0 else xr[:, it.par, j]
                    turn(take(it, e, tlo_done, i + 1), lambda k: src[:, k * P:(k + 1) * P], tr_done)
                if e[0] == "D":
                    y_ = e[1]
                    w = m * 2 + y_
                    wait(pe, tlo_done, m * 12 + 4 * y_ + NT)
                    wait(pe, wc_lo, w + 1)
                    mm3(take(it, e, relu_done, w + 1), lambda u, k: ws[:, u, 0, k * BK:(k + 1) * BK],
                        lambda v, k: ft[:, v, k], ks, dn_done)
                if e[0] == "U":
                    y_, j = e[1:]
                    i = m * 8 + 4 * y_ + j
                    wait(pe, zlo_done, m * 2 + y_ + 1)
                    mm3(take(it, e, yf_done, i + 1), lambda u, k: zs[:, u, j * P:(j + 1) * P],
                        lambda v, k: ws[:, v, 1], [(0, 0)], up_done)
                if e[0] == "CT":
                    j = e[1]
                    i = it.k * NT + j
                    wait(pe, s_done, (it.l - 1) * NT + j + 1)
                    turn(take(it, e, clo_done, i + 1), lambda k: s[:, j, k * P:(k + 1) * P], ctr_done)
                if e[0] == "PC":
                    mm_ = e[1]
                    n = it.k * NT + mm_
                    wait(pe, clo_done, it.k * NT + NT)
                    wait(pe, wtl_done, n + 1)
                    who = (pe_done if it.mix == "P" else qa_done, it.cg * NT + mm_ + 1)
                    mm3(take(it, e, *who), lambda u, k: wts[:, u, k], lambda v, k: ct[:, v, k], ks, pc_done)
                if e[0] == "GT":
                    j = e[1]
                    i = it.cg * NT + j
                    wait(pe, qg_done, it.cg * NT + NT)
                    turn(take(it, e, gy_done, i + 1), lambda k: pt[:, k, j * P:(j + 1) * P], gt_done)
                if e[0] == "ST":
                    n = it.l * FC + FC
                    wait(pe, sum_done, n)
                    wait(pe, sumsq_done, n)
                    bank = take(it, e, mom_done, it.l * 4 + 2)
                    for j in range(NT):
                        for w in range(2):
                            last = pe.matmul(bank[:, 2 * j + w:2 * j + w + 1], hsum[:, w, j * P:(j + 1) * P],
                                             ones[:, :], start=True, stop=True)
                    last.then_inc(stats_done, 1)

            pe.wait_ge(s_cst, 5)
            pre = It(0, -1, post=False)
            pre.bank = PRE_BANK
            for e in PRE:
                event(e, pre)
            for k in range(NT):
                pe.wait_ge(s_w2ld[k], 16)
            for b, col in ((0, be1c), (1, g1c)):
                for c in range(FC):
                    last = pe.matmul(phi[:, b], col[:, c:c + 1].to_broadcast([P, P]), late[:, c // NT, c % NT],
                                     start=(c == 0), stop=(c == FC - 1))
            last.then_inc(s_csum, 1)
            pe.wait_ge(s_wsl, NT + FC)

            def body(it):
                if it.post:
                    release.clear()
                    release[0] = (mom_done, it.l * 4 - 2)
                    release[1] = (tlo_done, it.l * 12 + 12)
                up_chunk(it.l, 0)
                for c in range(FC - 1):
                    up_chunk(it.l, c + 1)
                    for e in it.slots[c]:
                        event(e, it)
                    for j in range(NT):
                        down_tile(it, c, j)
                turns = [e for e in it.slots[FC - 1] if e[0] in USES_F]
                for e in turns[:2]:
                    event(e, it)
                for j in range(NT):
                    if j == NT - 1:
                        event(("ST",), it)
                    down_tile(it, FC - 1, j)
                    if 2 + j < len(turns):
                        event(turns[2 + j], it)

            iterations(pe, body)
            release.clear()
            release[0] = (mom_done, L * 4 - 2)
            for e in LAST_EVENTS:
                event(e, LAST)


_INS = ['x', 'condB_zX', 'condB_zY', 'condB_zR', 'itok_B_0_6', 'itok_B_0_8', 'condB_alphaparams',
        'L1_cond_down_w', 'L1_cond_down_b', 'L1_cond_up_w', 'L1_cond_up_b', 'L1_cond_ln_g', 'L1_cond_ln_b',
        'L2_cond_W1', 'L2_cond_b1', 'L2_cond_W2', 'L2_cond_b2', 'L2_cond_gamma', 'L2_cond_beta',
        'L3_cond_s_init', 'L3_cond_W1', 'L3_cond_b1', 'L3_cond_g1', 'L3_cond_be1', 'L3_cond_W2', 'L3_cond_b2',
        'L3_cond_g2', 'L3_cond_be2', 'L3_cond_Wt', 'L3_cond_bt', 'L3_cond_gt', 'L3_cond_bet']


def kernel(**inputs):
    import numpy as np
    import concourse.bacc as bacc
    from concourse.bass_utils import run_bass_kernel_spmd

    nc = bacc.Bacc("TRN2", target_bir_lowering=False, num_devices=1)
    arrays, args = {}, []
    for name in _INS:
        a = np.ascontiguousarray(inputs[name])
        arrays[f"in_{name}"] = a
        args.append(nc.dram_tensor(f"in_{name}", a.shape, mybir.dt.from_np(a.dtype), kind="ExternalInput").ap())
    args.append(nc.dram_tensor("out_0", (L, D, D), F32, kind="ExternalOutput").ap())
    build(nc, *args)
    r = run_bass_kernel_spmd(nc, [arrays], core_ids=[0])
    return r.results[0]["out_0"]
```

```python
from contextlib import ExitStack

import concourse.bass as bass
from concourse import mybir

ALU = mybir.AluOpType
ACT = mybir.ActivationFunctionType
F32 = mybir.dt.float32
F16 = mybir.dt.float16
I32 = mybir.dt.int32

P = 128
L = 16
D = 512
NT = D // P
BK = 128
F = 2048
FC = F // P
EVERY = 4
EPS = 1e-5
WS = 256.0

POST = {c: [("POST", c)] for c in range(NT)}
FRONT = {
    0: [("T", 0, 0)], 1: [("T", 0, 1)], 2: [("T", 0, 2)], 3: [("T", 0, 3), ("CW", 0), ("XB", 0, 0), ("XG", 0, 0)],
    4: [("D", 0)],
    5: [("U", 0, 0), ("XB", 0, 1), ("XG", 0, 1)],
    6: [("U", 0, 1), ("XB", 0, 2), ("XG", 0, 2), ("T", 1, 0)],
    7: [("U", 0, 2), ("XB", 0, 3), ("XG", 0, 3), ("T", 1, 1)],
    8: [("U", 0, 3), ("T", 1, 2)],
    9: [("T", 1, 3), ("CW", 1)],
    10: [("XB", 1, 0), ("XG", 1, 0), ("D", 1)],
    11: [("U", 1, 0), ("XB", 1, 1), ("XG", 1, 1)],
    12: [("U", 1, 1), ("XB", 1, 2), ("XG", 1, 2)],
    13: [("U", 1, 2), ("XB", 1, 3), ("XG", 1, 3)],
    14: [("U", 1, 3), ("T", 2, 0)],
    15: [("T", 2, 1), ("T", 2, 2), ("T", 2, 3)],
}
LZERO = {8: [("LP", 0)], 9: [("LP", 1), ("L0", 0)], 10: [("LP", 2), ("L0", 1)], 13: [("L0", 2)],
         14: [("LP", 3)], 15: [("L0", 3)]}
MIX = {
    1: [("CT", 0)], 2: [("CT", 1)], 3: [("CT", 2)], 4: [("CT", 3), ("WS", 0)],
    5: [("PC", 0), ("WS", 1)], 6: [("PC", 1), ("WS", 2)], 7: [("PC", 2), ("WS", 3)], 8: [("PC", 3)],
}
BACK = {9: [("GT", 0)], 10: [("GT", 1)], 11: [("GT", 2)], 12: [("GT", 3)],
        13: [("GO", 0)], 14: [("GO", 1)], 15: [("GO", 2), ("GO", 3)] + [("SC", j) for j in range(NT)]}
PREPARE = {
    3: [("W1", 0), ("W1", 1)], 5: [("CS", 0), ("CS", 1)], 6: [("CS", 2), ("CS", 3), ("CS", 4)],
    7: [("CS", 5), ("CS", 6), ("CS", 7), ("CS", 8)], 8: [("CS", c) for c in range(9, FC)] + [("LP", 0)],
    9: [("CA",), ("W1", 2), ("W1", 3), ("LP", 1), ("L0", 0)], 10: [("CB",), ("CM",), ("LP", 2), ("L0", 1)],
    14: [("LP", 3), ("CE", 0), ("CE", 1)],
    15: [("L0", 2), ("LO", 0), ("LO", 1), ("CE", 2), ("CE", 3), ("L0", 3)],
}
PREPARE_0 = {
    0: [("CE", 4), ("CE", 5), ("CE", 6), ("LO", 2), ("LO", 3)], 1: [("CE", 7), ("CE", 8), ("LO", 4), ("LO", 5)],
    2: [("CE", 9), ("CE", 10), ("LO", 6), ("LO", 7)], 3: [("CE", 11), ("CE", 12), ("LO", 8)],
    4: [("CE", 13), ("CE", 14), ("CE", 15), ("LO", 9), ("LO", 10)], 5: [("LO", 11)], 6: [("LO", 12)],
    7: [("LO", 13)], 8: [("LO", 14)], 9: [("LO", 15)],
}


BEHIND = ("XG", "LP", "L0", "GO", "SC", "CE")


def schedule(post, front, lzero, mix, more=()):
    parts = [POST] * post + [FRONT] * front + [LZERO] * lzero + [MIX] * (mix in "PQ") + [BACK] * (mix == "Q")
    parts += more
    return [sorted([e for part in parts for e in part.get(c, [])], key=lambda e: e[0] in BEHIND) for c in range(FC)]


EARLY = ("U",)
USES_F = ("T", "D", "U", "CT", "PC", "GT", "ST")


def f_banks(slots):
    uses = [e for slot in slots for e in slot if e[0] in USES_F] + [("ST",)]
    return {e: n % 2 for n, e in enumerate(uses)}


def build(nc, x, zx, zy, zr, id1, id2, alpha, dn_w1, dn_b1, up_w1, up_b1, ln_g1, ln_b1,
          dn_w2, dn_b2, up_w2, up_b2, ln_g2, ln_b2, s_init, w1, b1, g1, be1, w2, b2, g2, be2,
          wt, bt, gt, bet, out):
    dn_w, dn_b, up_w, up_b = (dn_w1, dn_w2), (dn_b1, dn_b2), (up_w1, up_w2), (up_b1, up_b2)
    ln_g, ln_b = (ln_g1, ln_g2), (ln_b1, ln_b2)
    n_ids = (dn_w1.shape[0], dn_w2.shape[0])

    with ExitStack() as ctx:
        def sb(name, shape, dt=F32):
            return ctx.enter_context(nc.sbuf_tensor(name, shape, dt))

        def sem(name):
            return ctx.enter_context(nc.semaphore(name))

        ctx.enter_context(nc.allow_non_contiguous_dma(reason="bias columns and weights by chunk, small"))

        w1s = sb("w1s", [P, 2, NT, F], F16)
        w2s = sb("w2s", [P, 2, FC, D], F16)
        xr = sb("xr", [P, 2, NT, D])
        x1 = sb("x1", [P, NT, D])
        x3t = sb("x3t", [P, 2, NT, D], F16)
        ft = sb("ft", [P, 2, NT, D], F16)
        xin = sb("xin", [P, NT + 2, D])
        z = sb("z", [P, D])
        zs = sb("zs", [P, 2, D], F16)
        wraw = sb("wraw", [P, 2, D])
        ws = sb("ws", [P, 2, 2, D], F16)
        dnb = sb("dnb", [P, 1])
        vec = sb("vec", [P, 3, D])
        xb = sb("xb", [P, D])
        y = sb("y", [P, D])
        late = sb("late", [P, 4, NT, D])
        y4, pt, s, ctf = (late[:, n] for n in range(4))
        ct = ctf.rearrange("p a b -> p (a b)").bitcast(F16).rearrange("p (h k d) -> p h k d", h=2, k=NT)
        rows = sb("rows", [P, 5, D])
        crow, g2r, be2r, gtr, betr = (rows[:, n] for n in range(5))
        hs = sb("hs", [P, 2, 2, D], F16)
        sq = sb("sq", [P, D])
        hsum = sb("hsum", [P, 2, D])
        la = sb("la", [P, 2, D])
        lh = sb("lh", [P, 2, D])
        wtr = sb("wtr", [P, 2, NT, P])
        wts = sb("wts", [P, 2, NT, P], F16)
        ident = sb("ident", [P, P])
        ones = sb("ones", [P, 1])
        nhalf = sb("nhalf", [P, NT])
        eps = sb("eps", [P, 1])
        ids = sb("ids", [1, 2, L], I32)
        cin = sb("cin", [P, 4, L])
        coef = sb("coef", [P, L, 6])
        c0 = sb("c0", [P, 6])
        ca = sb("ca", [P, 6])
        b1c = sb("b1c", [P, FC])
        bg1 = sb("bg1", [P, FC, 2])
        btc = sb("btc", [P, NT])
        mom = sb("mom", [P, NT, 2])
        msq = sb("msq", [P, NT])
        hvar = sb("hvar", [P, NT])
        rh = sb("rh", [P, NT])
        bn = sb("bn", [P, 6])
        mv = sb("mv", [P, 2])
        rs = sb("rs", [P, 1])
        bnp = sb("bnp", [P, 6])
        mvp = sb("mvp", [P, 2])
        rsp = sb("rsp", [P, 1])
        bng = sb("bng", [P, 6])
        mvg = sb("mvg", [P, 2])
        rsg = sb("rsg", [P, 1])

        phi = ctx.enter_context(nc.psum_tensor("phi", [P, NT, D], F32))
        hp = ctx.enter_context(nc.psum_tensor("hp", [P, 2, D], F32))
        fp = ctx.enter_context(nc.psum_tensor("fp", [P, 2, D], F32))

        s_cin = sem("s_cin")
        s_small = sem("s_small")
        s_ids = sem("s_ids")
        s_cst = sem("s_cst")
        s_coef = sem("s_coef")
        s_sig = sem("s_sig")
        s_step = sem("s_step")
        s_w1ld = [sem(f"s_w1ld{k}") for k in range(NT)]
        s_w2ld = [sem(f"s_w2ld{k}") for k in range(NT)]
        s_gw = sem("s_gw")
        s_w1h, s_w1l = sem("s_w1h"), sem("s_w1l")
        s_wsh, s_wsl = sem("s_wsh"), sem("s_wsl")
        s_csum = sem("s_csum")
        s_cs = sem("s_cs")
        s_cen = sem("s_cen")
        s_sld = sem("s_sld")
        w1_done, gelu_done, hi_done, sq_done = sem("w1_done"), sem("gelu_done"), sem("hi_done"), sem("sq_done")
        lo_done, sum_done, sumsq_done, w2_done = sem("lo_done"), sem("sum_done"), sem("sumsq_done"), sem("w2_done")
        phi_done = sem("phi_done")
        stats_done = sem("stats_done")
        ca_done, mom_done, rh_done = sem("ca_done"), sem("mom_done"), sem("rh_done")
        y2_done, bnp_done, mvp_done, s1_done = sem("y2_done"), sem("bnp_done"), sem("mvp_done"), sem("s1_done")
        s2_done, tp_done, rsp_done, s_done = sem("s2_done"), sem("tp_done"), sem("rsp_done"), sem("s_done")
        out_done = sem("out_done")
        st_done = sem("st_done")
        xin_ld = sem("xin_ld")
        raw_ld, vec_ld = sem("raw_ld"), sem("vec_ld")
        wc_hi, wc_lo = sem("wc_hi"), sem("wc_lo")
        tr_done, thi_done, tlo_done = sem("tr_done"), sem("thi_done"), sem("tlo_done")
        dn_done, relu_done, zhi_done, zlo_done = sem("dn_done"), sem("relu_done"), sem("zhi_done"), sem("zlo_done")
        up_done, yf_done, bnf_done, mvf_done = sem("up_done"), sem("yf_done"), sem("bnf_done"), sem("mvf_done")
        tf_done, rsf_done, xn_done = sem("tf_done"), sem("rsf_done"), sem("xn_done")
        xb_done, xg_done = sem("xb_done"), sem("xg_done")
        c0_done = sem("c0_done")
        l0v, l0h, l0a, l0q, l0s, l0x = (sem(n) for n in ("l0v", "l0h", "l0a", "l0q", "l0s", "l0x"))
        ctr_done, chi_done, clo_done = sem("ctr_done"), sem("chi_done"), sem("clo_done")
        wt_ld = [sem("wt_ld0"), sem("wt_ld1")]
        wth_done, wtl_done, pc_done = sem("wth_done"), sem("wtl_done"), sem("pc_done")
        pe_done = sem("pe_done")
        qa_done, qg_done = sem("qa_done"), sem("qg_done")
        qp_done = sem("qp_done")
        rb_done = sem("rb_done")
        xs_done = sem("xs_done")
        gt_done, gbn_done, gmv_done, gy_done = sem("gt_done"), sem("gbn_done"), sem("gmv_done"), sem("gy_done")
        grs_done, gs_done, go_done, sc_done = sem("grs_done"), sem("gs_done"), sem("go_done"), sem("sc_done")
        gst_done = sem("gst_done")

        def wait(eng, s_, value):
            if isinstance(value, int) and value <= 0:
                return
            eng.wait_ge(s_, value)

        def wait_split_free(eng, l, c):
            if c == 1:
                wait(eng, phi_done, l * NT)
            else:
                wait(eng, w2_done, l * (FC - 1) + max(c - 1, 0))

        def rows_of(ap):
            return ap.rearrange("(p r) d -> p r d", r=NT)

        class It:

            def __init__(self, g, j, post=True, front=True, lzero=True, mix="-", more=()):
                self.g, self.j, self.more = g, j, more
                self.l = g * EVERY + j
                self.post, self.front, self.lzero, self.mix = post, front, lzero, mix
                self.m = self.l + 1
                self.par = (j + 1) % 2
                self.slots = schedule(post, front, lzero, mix, more)
                self.bank = f_banks(self.slots)
                self.cg = g if mix == "P" else g - 1 if j == 0 else g
                self.k = self.cg * 2 + (mix == "Q")

        def has_up(it, c):
            return any(e[0] == "U" for e in it.slots[c])

        def stored(g, j):
            return g * (EVERY - 1) + j

        def iterations(eng, body):
            body(It(0, 0, post=False, more=[PREPARE_0]))
            body(It(0, 1))
            body(It(0, 2, mix="P"))
            body(It(0, 3))
            body(It(0, 4, mix="Q"))
            with eng.Fori(1, L // EVERY - 1) as g:
                body(It(g, 1))
                body(It(g, 2, mix="P"))
                body(It(g, 3))
                body(It(g, 4, mix="Q"))
            body(It(L // EVERY - 1, 1))
            body(It(L // EVERY - 1, 2, lzero=False, mix="P"))
            body(It(L // EVERY - 1, 3, front=False, lzero=False, more=[SPLIT_WT]))

        PRE = It(0, -1, post=False, lzero=False, more=[PREPARE])
        PRE_EVENTS = [e for slot in PRE.slots for e in slot]
        w1_place = [xr[:, 1].rearrange("p a b -> p (a b)"), x3t.rearrange("p a b c -> p (a b c)").bitcast(F32)]
        w1_raw = [w1_place[k % 2] for k in range(NT)]
        w2_raw = [late[:, c // NT, c % NT] for c in range(FC)]
        sums, mean = sq[0:2, :], betr
        LAST = It(L // EVERY - 1, 4, front=False, lzero=False, mix="Q")
        LAST_EVENTS = [("POST", 0), ("POST", 1), ("CT", 0), ("POST", 2), ("CT", 1), ("POST", 3), ("CT", 2),
                       ("RB", 0), ("RB", 1), ("RB", 2), ("RB", 3), ("QP", 0), ("CT", 3), ("QP", 1), ("GT", 0),
                       ("QP", 2), ("GT", 1), ("QP", 3), ("GT", 2), ("GT", 3)]
        SPLIT_WT = {c: [("WF", c - 1)] for c in range(1, NT + 1)}
        LAST.bank = f_banks([LAST_EVENTS])

        block = ctx.enter_context(nc.Block())

        @block.sync
        def _(sp):
            def load_x(m, free):
                if free is not None:
                    sp.wait_ge(l0x, free)
                src = x[m] if isinstance(m, int) else x[bass.ds(m, 1)].rearrange("a r d -> (a r) d")
                for dst, rws in ((xin[:, 1:NT + 1], rows_of(src)),
                                 (xin[1:P - 1, 0], src[3:D - 8:NT]), (xin[P - 1:P, 0], src[D - 5:D - 4]),
                                 (xin[0:1, 0], src[1:2]),
                                 (xin[0:P - 2, NT + 1], src[NT:D - 4:NT]), (xin[P - 2:P - 1, NT + 1], src[D - 4:D - 3]),
                                 (xin[P - 1:P, NT + 1], src[D - 2:D - 1])):
                    sp.dma_start(dst, rws).then_inc(xin_ld, 16)

            def pick(y_, m):
                i = ids[0:1, y_, m:m + 1] if isinstance(m, int) else ids[0:1, y_, bass.ds(m, 1)]
                return sp.value_load(i, min_val=0, max_val=n_ids[y_] - 1)

            def load_raw(m, y_):
                i = pick(y_, m)
                wait(sp, wc_lo, m * 2 + y_)
                sp.dma_start(wraw[:, 0].rearrange("p (k b) -> p k b", k=NT),
                             dn_w[y_][bass.ds(i, 1)].rearrange("a (k p) b -> p (a k) b", p=P)).then_inc(raw_ld, 16)
                sp.dma_start(wraw[:, 1], up_w[y_][bass.ds(i, 1)].rearrange("a k d -> (a k) d")).then_inc(raw_ld, 16)

            def load_vec(m, y_):
                i = pick(y_, m)
                wait(sp, xn_done, (m * 2 + y_) * NT)
                for n, t in enumerate((up_b[y_], ln_g[y_], ln_b[y_])):
                    sp.dma_start(vec[:, n], t[bass.ds(i, 1)].to_broadcast([P, D])).then_inc(vec_ld, 16)
                sp.dma_start(dnb[:, :], dn_b[y_][bass.ds(i, 1)].rearrange("a p -> p a")).then_inc(vec_ld, 16)

            for n, t in enumerate((id1, id2)):
                sp.dma_start(ids[:, n], t.rearrange("(a n) -> a n", a=1)).then_inc(s_ids, 16)
            for n, t in enumerate((zx, zy, zr, alpha)):
                sp.dma_start(cin[:, n], t.rearrange("(a n) -> a n", a=1).to_broadcast([P, L])).then_inc(s_cin, 16)
            load_x(0, None)
            sp.wait_ge(s_ids, 32)
            load_raw(0, 0)
            load_vec(0, 0)
            for dst, t in ((bg1[:, :, 0], be1), (bg1[:, :, 1], g1), (b1c[:, :], b1)):
                sp.dma_start(dst, t.rearrange("(c p) -> p c", p=P)).then_inc(s_small, 16)
            sp.dma_start(btc[:, :], bt.rearrange("(c p) -> p c", p=P)).then_inc(s_small, 16)
            for n, t in enumerate((b2, g2, be2, gt)):
                sp.dma_start(rows[:, n], t.rearrange("(a n) -> a n", a=1).to_broadcast([P, D])).then_inc(s_small, 16)
            load_x(1, NT)
            for k in (2, 3):
                sp.wait_ge(s_w1l, k - 1)
                sp.dma_start(w1_raw[k], w1[k * P:(k + 1) * P, :]).then_inc(s_w1ld[k], 16)
            load_raw(0, 1)
            load_vec(0, 1)
            load_raw(1, 0)

            def load_state():
                sp.wait_ge(s_wsl, FC)
                sp.dma_start(s, rows_of(s_init)).then_inc(s_sld, 16)
                sp.dma_start(betr, bet.rearrange("(a n) -> a n", a=1).to_broadcast([P, D])).then_inc(s_sld, 16)

            def body(it):
                if it.lzero:
                    load_x(it.m + 1, (it.m + 1) * NT)
                if it.front:
                    load_vec(it.m, 0)
                    load_raw(it.m, 1)
                n, jl = stored(it.g, it.j - 1), it.j - 1
                if it.post and jl % EVERY != EVERY - 1:
                    store(n, it.l - 1, jl % 2)
                if it.front:
                    load_vec(it.m, 1)
                if PREPARE_0 in it.more:
                    load_state()
                if it.lzero:
                    load_raw(it.m + 1, 0)
                if it.mix == "Q":
                    store_ck(it)

            def store(n, l, par):
                dst = out[l] if isinstance(l, int) else out[bass.ds(l, 1)].rearrange("a r d -> (a r) d")
                for j in range(NT):
                    sp.wait_ge(out_done, n * NT + j + 1)
                    sp.dma_start(rows_of(dst)[:, j], xr[:, par, j]).then_inc(st_done, 16)

            def store_ck(it):
                l = it.l - 1
                dst = out[l] if isinstance(l, int) else out[bass.ds(l, 1)].rearrange("a r d -> (a r) d")
                for j in range(NT):
                    if it is LAST:
                        sp.wait_ge(gs_done, it.cg * NT + j + 1)
                        sp.dma_start(rows_of(dst)[:, j], xr[:, 1, j]).then_inc(gst_done, 16)
                    else:
                        sp.wait_ge(go_done, it.cg * NT + j + 1)
                        sp.dma_start(rows_of(dst)[:, j], pt[:, j]).then_inc(gst_done, 16)

            iterations(sp, body)
            store_ck(LAST)
            sp.wait_ge(st_done, 64 * (L - L // EVERY))
            sp.wait_ge(gst_done, 64 * (L // EVERY))

        @block.gpsimd
        def _(pool):
            def tt(out_, a, b, op, done):
                pool.tensor_tensor(out_, a, b, op).then_inc(done, 1)

            def rstd(dst, src, n, done):
                tt(dst, src, eps[:, :], ALU.add, done)
                pool.wait_ge(done, n + 1)
                tt(dst, dst, nhalf[:, 0:1], ALU.pow, done)

            def event(e, it):
                m = it.m
                if e[0] == "CE":
                    w = w2_raw[e[1]]
                    pool.wait_ge(s_gw, e[1] + 1)
                    pool.wait_ge(s_cs, 3)
                    tt(w, w, mean, ALU.subtract, s_cen)
                if e[0] == "RB":
                    tt(xr[:, 1, e[1]], xr[:, 1, e[1]], betr, ALU.add, rb_done)
                if e[0] == "XB":
                    y_, j = e[1:]
                    i = m * 8 + 4 * y_ + j
                    src = x1[:, j] if y_ == 0 else xr[:, it.par, j]
                    if y_ == 0:
                        pool.wait_ge(l0x, m * NT + j + 1)
                    else:
                        pool.wait_ge(xn_done, m * 8 + j + 1)
                        pool.wait_ge(tr_done, m * 12 + NT + j + 1)
                    pool.wait_ge(vec_ld, (m * 2 + y_ + 1) * 64)
                    wait(pool, yf_done, i)
                    tt(xb[:, :], src, vec[:, 0], ALU.add, xb_done)
                if e[0] == "XG":
                    y_, j = e[1:]
                    src = x1[:, j] if y_ == 0 else xr[:, it.par, j]
                    if y_ == 0:
                        free_xr(it)
                    tt(xr[:, it.par, j], src, vec[:, 2], ALU.add, xg_done)
                if e[0] == "U":
                    y_, j = e[1:]
                    i = m * 8 + 4 * y_ + j
                    pool.wait_ge(mvf_done, i + 1)
                    rstd(rs[:, :], mv[:, 1:2], i * 2, rsf_done)
                if e[0] == "POST":
                    l, j = it.l - 1, e[1]
                    i = l * NT + j
                    pool.wait_ge(mvp_done, i + 1)
                    rstd(rsp[:, :], mvp[:, 1:2], i * 3, rsp_done)
                    pool.wait_ge(rsp_done, i * 3 + 2)
                    tt(rsp[:, :], rsp[:, :], ca[:, 4:5], ALU.mult, rsp_done)
                    if it.j % EVERY != 0:
                        pool.wait_ge(s_done, i + 1)
                        r = xr[:, (it.j - 1) % 2, j]
                        tt(r, r, s[:, j], ALU.add, out_done)
                if e[0] == "LP":
                    lap(m + 1, e[1])
                if e[0] == "GT":
                    i = it.cg * NT + e[1]
                    pool.wait_ge(gmv_done, i + 1)
                    rstd(rsg[:, :], mvg[:, 1:2], i * 2, grs_done)
                if e[0] == "GO":
                    i = it.cg * NT + e[1]
                    pool.wait_ge(gs_done, i + 1)
                    pool.wait_ge(xs_done, i + 1)
                    pool.wait_ge(gt_done, (it.cg + 1) * NT)
                    tt(pt[:, e[1]], y4[:, e[1]], s[:, e[1]], ALU.add, go_done)

            def free_xr(it):
                jp = it.j - 1
                if jp < 0:
                    if it.par == 1:
                        pool.wait_ge(s_w1l, NT - 1)
                    return
                if jp % EVERY != EVERY - 1:
                    pool.wait_ge(st_done, (stored(it.g, jp) + 1) * 64)
                else:
                    pool.wait_ge(xs_done, (it.cg + 1) * NT)

            def lap(m, r):
                i, b = m * NT + r, r % 2
                if r == 0:
                    pool.wait_ge(xin_ld, (m + 1) * 112)
                wait(pool, tlo_done, 12 * (m - 1) + r + 1)
                wait(pool, xg_done, 8 * (m - 1) + r + 1)
                tt(x1[:, r], xin[:, r], xin[:, r + 2], ALU.add, l0v)
                wait(pool, l0x, i - 1)
                c = xin[:, r + 1]
                if not (isinstance(m, int) and m == 0):
                    tt(lh[:, b, 1:D - 1], c[:, 0:D - 2], c[:, 2:D], ALU.add, l0h)
                    tt(lh[:, b, 0:D:D - 1], c[:, 1:D - 1:D - 3], c[:, 1:D - 1:D - 3], ALU.add, l0h)
                pool.wait_ge(l0a, i + 1)
                tt(la[:, b], la[:, b], c, ALU.mult, l0q)

            pool.memset(ident[:, :], 0.0).then_inc(s_cst, 1)
            pool.memset(ones[:, :], 1.0).then_inc(s_cst, 1)
            pool.memset(nhalf[:, :], -0.5).then_inc(s_cst, 1)
            pool.memset(eps[:, :], EPS).then_inc(s_cst, 1)
            pool.wait_ge(s_cst, 4)
            pool.affine_select(out=ident[:, :], in_=ident[:, :], compare_op=ALU.not_equal, fill=1.0, base=0,
                               pattern=[[-1, P]], channel_multiplier=1).then_inc(s_cst, 1)
            for r in range(NT):
                lap(0, r)
            for e in PRE_EVENTS:
                event(e, PRE)

            def rh_step(l):
                pool.wait_ge(mom_done, l * 4 + 4)
                tt(rh[:, :], hvar[:, :], nhalf[:, :], ALU.pow, rh_done)

            def body(it):
                if it.post:
                    rh_step(it.l - 1)
                for c in range(FC):
                    for e in it.slots[c]:
                        event(e, it)

            iterations(pool, body)
            rh_step(L - 1)
            for e in LAST_EVENTS:
                event(e, LAST)

        @block.scalar
        def _(act):
            def copy(out_, in_, done, scale=1.0):
                act.activation(out_, in_, ACT.Copy, scale=scale).then_inc(done, 1)

            def gelu_step(n, c):
                act.wait_ge(w1_done, n + 1)
                act.activation(hp[:, c % 2], hp[:, c % 2], ACT.Gelu, bias=b1c[:, c:c + 1],
                               scale=1.0 / WS).then_inc(gelu_done, 1)

            def hi_step(l, n, c):
                act.wait_ge(gelu_done, n + 1)
                wait_split_free(act, l, c)
                copy(hs[:, c % 2, 0], hp[:, c % 2], hi_done)
                wait(act, sumsq_done, n)
                act.activation(sq[:, :], hp[:, c % 2], ACT.Square).then_inc(sq_done, 1)

            def event(e, it):
                m, bank = it.m, it.bank.get(e)
                if e[0] == "W1":
                    w1_hi(e[1])
                if e[0] == "CE":
                    act.wait_ge(s_csum, 1)
                    copy(w2_raw[e[1]], w2_raw[e[1]], s_gw, scale=bg1[:, e[1], 1:2])
                if e[0] == "LO":
                    act.wait_ge(s_cen, e[1] + 1)
                    copy(w2s[:, 0, e[1]], w2_raw[e[1]], s_wsh, scale=WS)
                if e[0] == "T":
                    t, j = e[1:]
                    i = m * 12 + 4 * t + j
                    act.wait_ge(tr_done, i + 1)
                    dst = x3t if t == 2 else ft
                    if t == 2 and it is PRE:
                        act.wait_ge(s_w1l, NT)
                    elif t == 2:
                        act.wait_ge(w1_done, m * FC)
                    else:
                        wait(act, dn_done, m * 2 + t)
                    copy(dst[:, 0, :, j * P:(j + 1) * P], fp[:, bank].rearrange("p (k q) -> p k q", k=NT), thi_done)
                if e[0] == "CW":
                    w = m * 2 + e[1]
                    act.wait_ge(raw_ld, (w + 1) * 32)
                    wait(act, up_done, w * NT)
                    copy(ws[:, 0], wraw[:, :], wc_hi, scale=WS)
                if e[0] == "D":
                    w = m * 2 + e[1]
                    act.wait_ge(dn_done, w + 1)
                    act.wait_ge(vec_ld, (w + 1) * 64)
                    wait(act, zlo_done, w)
                    act.activation(z[:, :], fp[:, bank], ACT.Relu, bias=dnb[:, 0:1], scale=1.0 / WS)\
                       .then_inc(relu_done, 1)
                    act.wait_ge(relu_done, w + 1)
                    wait(act, up_done, w * NT)
                    copy(zs[:, 0], z[:, :], zhi_done)
                if e[0] == "POST":
                    l, j = it.l - 1, e[1]
                    i = l * NT + j
                    act.wait_ge(ca_done, l + 1)
                    s_before(it, l, j)
                    act.activation(s[:, j], s[:, j], ACT.Copy, scale=ca[:, 5:6]).then_inc(s1_done, 1)
                if e[0] == "LP":
                    lap(m + 1, e[1])
                if e[0] == "CT":
                    i = it.k * NT + e[1]
                    act.wait_ge(ctr_done, i + 1)
                    wait(act, pc_done, it.k * NT)
                    copy(ct[:, 0, :, e[1] * P:(e[1] + 1) * P], fp[:, bank].rearrange("p (k q) -> p k q", k=NT),
                         chi_done)
                    if it is LAST:
                        return
                    if it.mix == "Q":
                        copy(s[:, e[1]], xr[:, 1, e[1]], xs_done)
                    if e[1] == NT - 2:
                        load_wt(it, 0)
                        load_wt(it, 1)
                if e[0] == "WS":
                    n = it.k * NT + e[1]
                    act.wait_ge(wt_ld[e[1] % 2], (it.k * 2 + e[1] // 2 + 1) * 16)
                    wait(act, pc_done, n)
                    copy(wts[:, 0], wtr[:, e[1] % 2], wth_done, scale=WS)
                if e[0] == "PC":
                    n = it.k * NT + e[1]
                    if e[1] + 2 < NT:
                        load_wt(it, e[1] + 2)
                    if it.mix == "P":
                        act.wait_ge(pc_done, n + 1)
                        wait(act, gst_done, it.cg * 64)
                        copy(pt[:, e[1]], fp[:, bank], pe_done, scale=1.0 / WS)
                    else:
                        i = it.cg * NT + e[1]
                        act.wait_ge(qa_done, i + 1)
                        act.activation(pt[:, e[1]], pt[:, e[1]], ACT.Gelu, bias=btc[:, e[1]:e[1] + 1])\
                           .then_inc(qg_done, 1)
                if e[0] == "WF":
                    if e[1] == 0:
                        load_wt(LAST, 0)
                        load_wt(LAST, 1)
                    n = LAST.k * NT + e[1]
                    act.wait_ge(wt_ld[e[1] % 2], (LAST.k * 2 + e[1] // 2 + 1) * 16)
                    act.wait_ge(dn_done, L * 2)
                    copy(ft[:, 0, e[1]].rearrange("p (k n) -> p k n", k=NT), wtr[:, e[1] % 2], wth_done, scale=WS)
                    if e[1] + 2 < NT:
                        load_wt(LAST, e[1] + 2)
                if e[0] == "QP":
                    i = it.cg * NT + e[1]
                    act.wait_ge(qa_done, i + 1)
                    for k in range(NT):
                        v = pt[:, k, e[1] * P:(e[1] + 1) * P]
                        act.activation(v, v, ACT.Gelu, bias=btc[:, k:k + 1]).then_inc(qp_done, 1)
                if e[0] == "SC":
                    i = it.cg * NT + e[1]
                    act.wait_ge(go_done, i + 1)
                    copy(s[:, e[1]], y4[:, e[1]], sc_done)

            def load_wt(it, mm):
                n = it.k * NT + mm
                half = D if it.mix == "P" else 0
                wait(act, wtl_done, n - 1)
                act.dma_start(wtr[:, mm % 2], wt[half:half + D, mm * P:(mm + 1) * P]
                              .rearrange("(k p) n -> p k n", p=P)).then_inc(wt_ld[mm % 2], 16)

            def s_before(it, l, j):
                prev = (it.j - 2) % EVERY
                if isinstance(it.l, int) and it.l == 1:
                    act.wait_ge(s_sld, 32)
                    return
                if prev == EVERY - 1:
                    q = it.g if it.j == 1 else it.g + 1
                    if j == 0:
                        act.wait_ge(sc_done, q * NT)
                else:
                    n = stored(it.g, it.j - 2)
                    act.wait_ge(s_done, l * NT - NT + j + 1)
                    act.wait_ge(out_done, n * NT + j + 1)
                    if prev == 1:
                        act.wait_ge(ctr_done, it.g * 8 + j + 1)

            def lap(n, r):
                i = n * NT + r
                act.wait_ge(c0_done, n + 1)
                act.wait_ge(xin_ld, (n + 1) * 112)
                wait(act, l0x, i - 1)
                act.activation(la[:, r % 2], xin[:, r + 1], ACT.Identity, bias=c0[:, 0:1], scale=c0[:, 1:2])\
                   .then_inc(l0a, 1)

            def w1_hi(k):
                act.wait_ge(s_w1ld[k], 16)
                copy(w1s[:, 0, k], w1_raw[k], s_w1h, scale=WS)

            act.wait_ge(s_cin, 4 * 16)
            act.wait_ge(s_coef, 4)
            act.activation(coef[:, :, 4], cin[:, 3], ACT.Sigmoid).then_inc(s_sig, 1)
            lap(0, 0)
            lap(0, 1)
            act.wait_ge(xin_ld, 112)
            act.wait_ge(raw_ld, 32)
            act.wait_ge(vec_ld, 64)
            for k in (0, 1):
                act.dma_start(w1_raw[k], w1[k * P:(k + 1) * P, :]).then_inc(s_w1ld[k], 16)
            for k in range(NT):
                act.dma_start(late[:, k], w2.rearrange("(q c p) d -> q p c d", p=P, q=NT)[k]).then_inc(s_w2ld[k], 16)
            lap(0, 2)
            lap(0, 3)
            for e in PRE_EVENTS:
                event(e, PRE)
            act.wait_ge(s_small, 8 * 16)

            def body(it):
                n = it.l * FC
                gelu_step(n, 0)
                hi_step(it.l, n, 0)
                for c in range(FC):
                    if c + 1 < FC:
                        gelu_step(n + c + 1, c + 1)
                    if has_up(it, c):
                        hi_step(it.l, n + c + 1, c + 1)
                    for e in it.slots[c]:
                        event(e, it)
                    if c + 1 < FC and not has_up(it, c):
                        hi_step(it.l, n + c + 1, c + 1)

            iterations(act, body)
            for e in LAST_EVENTS:
                event(e, LAST)

        @block.vector
        def _(dve):
            def stt(out_, a, sc, b, op0, op1, done):
                dve.scalar_tensor_tensor(out_, a, sc, b, op0, op1).then_inc(done, 1)

            def aggr(out_, in_, bn_sem, n, done):
                dve.wait_ge(bn_sem, n)
                dve.sem_inc(s_step)
                dve.bn_aggr(out_, in_).then_inc(done, 1)

            def lo(it, c):
                n, b = it.l * FC + c, c % 2
                dve.wait_ge(hi_done, n + 1)
                dve.wait_ge(sq_done, n + 1)
                wait_split_free(dve, it.l, c)
                stt(hs[:, b, 1], hp[:, b], 1.0, hs[:, b, 0], ALU.mult, ALU.subtract, lo_done)

            def add_h(it, c):
                n = it.l * FC + c
                if c == 0:
                    wait(dve, stats_done, it.l)
                    dve.tensor_copy(hsum[:, 0], hp[:, 0]).then_inc(sum_done, 1)
                else:
                    dve.wait_ge(sum_done, n)
                    dve.tensor_tensor(hsum[:, 0], hp[:, c % 2], hsum[:, 0], ALU.add).then_inc(sum_done, 1)

            def add_h2(it, c):
                n = it.l * FC + c
                if c == 0:
                    dve.tensor_copy(hsum[:, 1], sq[:, :]).then_inc(sumsq_done, 1)
                else:
                    dve.wait_ge(sumsq_done, n)
                    dve.tensor_tensor(hsum[:, 1], hsum[:, 1], sq[:, :], ALU.add).then_inc(sumsq_done, 1)

            def moments(it, l, bank):
                st = fp[:, bank, 0:2 * NT].rearrange("p (j w) -> p j w", w=2)
                wait(dve, rsp_done, l * NT * 3)
                wait(dve, s2_done, l * NT)
                row = coef[:, l] if isinstance(l, int) else coef[:, bass.ds(l, 1)].rearrange("p a n -> p (a n)")
                dve.sem_inc(s_step)
                dve.tensor_copy(ca[:, :], row).then_inc(ca_done, 1)
                dve.wait_ge(stats_done, l + 1)
                wait(dve, y2_done, l * NT)
                i = l * 4
                dve.tensor_scalar(mom[:, :, 0], st[:, :, 0], WS / F, None, ALU.mult).then_inc(mom_done, 1)
                dve.tensor_scalar(mom[:, :, 1], st[:, :, 1], WS * WS / F, WS * WS * EPS, ALU.mult, ALU.add)\
                   .then_inc(mom_done, 1)
                dve.wait_ge(mom_done, i + 2)
                dve.tensor_tensor(msq[:, :], mom[:, :, 0], mom[:, :, 0], ALU.mult).then_inc(mom_done, 1)
                dve.wait_ge(mom_done, i + 3)
                wait(dve, rh_done, l)
                dve.tensor_tensor(hvar[:, :], mom[:, :, 1], msq[:, :], ALU.subtract).then_inc(mom_done, 1)
                dve.wait_ge(rh_done, l + 1)
                if it is not LAST:
                    for j in range(NT):
                        hidden_ln(it, l, j)

            def hidden_ln(it, l, j):
                dve.wait_ge(phi_done, l * NT + j + 1)
                y4_free(it, l, j)
                stt(y4[:, j], phi[:, j], rh[:, j:j + 1], crow, ALU.mult, ALU.add, y2_done)

            def y4_free(it, l, j):
                if isinstance(it.l, int) and it.l == 1:
                    return
                dve.wait_ge(s_done, (l - 1) * NT + j + 1)
                if (it.j - 2) % EVERY == EVERY - 1:
                    q = it.g if it.j == 1 else it.g + 1
                    dve.wait_ge(sc_done, q * NT)

            def event(e, it):
                m, bank = it.m, it.bank.get(e)
                if e[0] == "W1":
                    k = e[1]
                    dve.wait_ge(s_w1h, k + 1)
                    stt(w1s[:, 1, k], w1_raw[k], WS, w1s[:, 0, k], ALU.mult, ALU.subtract, s_w1l)
                if e[0] == "CA":
                    dve.wait_ge(s_csum, 1)
                    dve.tensor_copy(sums, phi[0:2, 0]).then_inc(s_cs, 1)
                if e[0] == "CM":
                    dve.wait_ge(s_csum, 2)
                    dve.wait_ge(s_small, 8 * 16)
                    dve.tensor_tensor(crow, phi[:, 1], crow, ALU.add).then_inc(s_cs, 1)
                    dve.tensor_scalar(mean, phi[:, 2], 1.0 / F, None, ALU.mult).then_inc(s_cs, 1)
                if e[0] == "LO":
                    dve.wait_ge(s_wsh, e[1] + 1)
                    stt(w2s[:, 1, e[1]], w2_raw[e[1]], WS, w2s[:, 0, e[1]], ALU.mult, ALU.subtract, s_wsl)
                if e[0] == "T":
                    t, j = e[1:]
                    i = m * 12 + 4 * t + j
                    dve.wait_ge(thi_done, i + 1)
                    dst = x3t if t == 2 else ft
                    cols = slice(j * P, (j + 1) * P)
                    stt(dst[:, 1, :, cols], fp[:, bank].rearrange("p (k q) -> p k q", k=NT), 1.0, dst[:, 0, :, cols],
                        ALU.mult, ALU.subtract, tlo_done)
                if e[0] == "CW":
                    w = m * 2 + e[1]
                    dve.wait_ge(wc_hi, w + 1)
                    stt(ws[:, 1], wraw[:, :], WS, ws[:, 0], ALU.mult, ALU.subtract, wc_lo)
                if e[0] == "D":
                    w = m * 2 + e[1]
                    dve.wait_ge(zhi_done, w + 1)
                    stt(zs[:, 1], z[:, :], 1.0, zs[:, 0], ALU.mult, ALU.subtract, zlo_done)
                if e[0] == "POST":
                    l, j = it.l - 1, e[1]
                    i = l * NT + j
                    if it is LAST:
                        hidden_ln(it, l, j)
                    dve.wait_ge(y2_done, i + 1)
                    dve.bn_stats(bnp[:, :], y4[:, j]).then_inc(bnp_done, 1)
                    wait(dve, rsp_done, i * 3)
                    aggr(mvp[:, :], bnp[:, :], bnp_done, i + 1, mvp_done)
                    dve.wait_ge(s1_done, i + 1)
                    stt(s[:, j], be2r, ca[:, 4:5], s[:, j], ALU.mult, ALU.add, s2_done)
                    dve.wait_ge(mvp_done, i + 1)
                    stt(y4[:, j], y4[:, j], mvp[:, 0:1], g2r, ALU.subtract, ALU.mult, tp_done)
                    dve.wait_ge(tp_done, i + 1)
                    dve.wait_ge(s2_done, i + 1)
                    dve.wait_ge(rsp_done, i * 3 + 3)
                    stt(s[:, j], y4[:, j], rsp[:, 0:1], s[:, j], ALU.mult, ALU.add, s_done)
                if e[0] == "L0":
                    lap(m + 1, e[1])
                if e[0] == "CT":
                    i = it.k * NT + e[1]
                    cols = slice(e[1] * P, (e[1] + 1) * P)
                    dve.wait_ge(chi_done, i + 1)
                    stt(ct[:, 1, :, cols], fp[:, bank].rearrange("p (k q) -> p k q", k=NT), 1.0, ct[:, 0, :, cols],
                        ALU.mult, ALU.subtract, clo_done)
                if e[0] == "WS":
                    n = it.k * NT + e[1]
                    dve.wait_ge(wth_done, n + 1)
                    stt(wts[:, 1], wtr[:, e[1] % 2], WS, wts[:, 0], ALU.mult, ALU.subtract, wtl_done)
                if e[0] == "WF":
                    n = LAST.k * NT + e[1]
                    dve.wait_ge(wth_done, n + 1)
                    stt(ft[:, 1, e[1]].rearrange("p (k n) -> p k n", k=NT), wtr[:, e[1] % 2], WS,
                        ft[:, 0, e[1]].rearrange("p (k n) -> p k n", k=NT), ALU.mult, ALU.subtract, wtl_done)
                if e[0] == "QP":
                    j = e[1]
                    dve.wait_ge(pc_done, it.k * NT + j + 1)
                    dve.wait_ge(pe_done, (it.cg + 1) * NT)
                    v = pt[:, :, j * P:(j + 1) * P]
                    stt(v, phi[:, j].rearrange("p (k q) -> p k q", k=NT), 1.0 / WS, v, ALU.mult, ALU.add, qa_done)
                if e[0] == "PC" and it.mix == "Q":
                    i = it.cg * NT + e[1]
                    dve.wait_ge(pc_done, it.k * NT + e[1] + 1)
                    dve.wait_ge(pe_done, i + 1)
                    stt(pt[:, e[1]], fp[:, bank], 1.0 / WS, pt[:, e[1]], ALU.mult, ALU.add, qa_done)
                if e[0] == "GT":
                    j = e[1]
                    i = it.cg * NT + j
                    dve.wait_ge(gt_done, i + 1)
                    dve.bn_stats(bng[:, :], fp[:, bank]).then_inc(gbn_done, 1)
                    wait(dve, grs_done, i * 2)
                    aggr(mvg[:, :], bng[:, :], gbn_done, i + 1, gmv_done)
                    dve.wait_ge(gmv_done, i + 1)
                    dve.wait_ge(s_done, (it.l - 1) * NT + j + 1)
                    stt(y4[:, j], fp[:, bank], mvg[:, 0:1], gtr, ALU.subtract, ALU.mult, gy_done)
                    dve.wait_ge(gy_done, i + 1)
                    dve.wait_ge(grs_done, i * 2 + 2)
                    if it is LAST:
                        dve.wait_ge(rb_done, j + 1)
                        stt(xr[:, 1, j], y4[:, j], rsg[:, 0:1], xr[:, 1, j], ALU.mult, ALU.add, gs_done)
                    else:
                        stt(y4[:, j], y4[:, j], rsg[:, 0:1], betr, ALU.mult, ALU.add, gs_done)

            def up(it, e, c=None):
                y_, j = e[1:]
                i, bank = it.m * 8 + 4 * y_ + j, it.bank[e]
                dve.wait_ge(up_done, i + 1)
                dve.wait_ge(xb_done, i + 1)
                wait(dve, xn_done, i)
                stt(y[:, :], fp[:, bank], 1.0 / WS, xb[:, :], ALU.mult, ALU.add, yf_done)
                if c is not None:
                    add_h(it, c)
                dve.wait_ge(yf_done, i + 1)
                dve.bn_stats(bn[:, :], y[:, :]).then_inc(bnf_done, 1)
                if c is not None:
                    add_h2(it, c)
                wait(dve, rsf_done, i * 2)
                aggr(mv[:, :], bn[:, :], bnf_done, i + 1, mvf_done)
                dve.wait_ge(mvf_done, i + 1)
                stt(y[:, :], y[:, :], mv[:, 0:1], vec[:, 1], ALU.subtract, ALU.mult, tf_done)
                if c is not None:
                    lo(it, c + 1)
                dve.wait_ge(tf_done, i + 1)
                dve.wait_ge(rsf_done, i * 2 + 2)
                dve.wait_ge(xg_done, i + 1)
                r = xr[:, it.par, j]
                stt(r, y[:, :], rs[:, 0:1], r, ALU.mult, ALU.add, xn_done)

            def lap(n, r):
                i = n * NT + r
                dve.wait_ge(l0q, i + 1)
                a, b = la[:, r % 2], lh[:, r % 2]
                stt(a, x1[:, r], c0[:, 3:4], a, ALU.mult, ALU.add, l0s)
                dve.wait_ge(l0s, i + 1)
                stt(x1[:, r], b, c0[:, 2:3], a, ALU.mult, ALU.add, l0x)

            def pick_c0(n):
                wait(dve, l0x, n * NT)
                dve.sem_inc(s_step)
                row = coef[:, n] if isinstance(n, int) else coef[:, bass.ds(n, 1)].rearrange("p a n -> p (a n)")
                dve.tensor_copy(c0[:, :], row).then_inc(c0_done, 1)

            dve.wait_ge(s_cin, 4 * 16)
            dve.tensor_tensor(coef[:, :, 0], cin[:, 0], cin[:, 1], ALU.add).then_inc(s_coef, 1)
            dve.tensor_scalar(coef[:, :, 1], cin[:, 2], -1.0, None, ALU.mult).then_inc(s_coef, 1)
            dve.tensor_copy(coef[:, :, 2], cin[:, 0]).then_inc(s_coef, 1)
            dve.tensor_copy(coef[:, :, 3], cin[:, 1]).then_inc(s_coef, 1)
            dve.wait_ge(s_coef, 4)
            dve.tensor_scalar(coef[:, :, 0], coef[:, :, 0], -2.0, 1.0, ALU.mult, ALU.add).then_inc(s_coef, 1)
            dve.wait_ge(s_coef, 5)
            dve.tensor_tensor(coef[:, :, 0], coef[:, :, 0], cin[:, 2], ALU.add).then_inc(s_coef, 1)
            dve.wait_ge(s_sig, 1)
            dve.tensor_scalar(coef[:, :, 5], coef[:, :, 4], -1.0, 1.0, ALU.mult, ALU.add).then_inc(s_coef, 1)
            dve.wait_ge(s_coef, 7)
            pick_c0(0)
            dve.wait_ge(xin_ld, 112)
            for r in range(NT):
                a, c = lh[:, r % 2], xin[:, r + 1]
                dve.tensor_tensor(a[:, 1:D - 1], c[:, 0:D - 2], c[:, 2:D], ALU.add).then_inc(l0h, 1)
                dve.tensor_tensor(a[:, 0:D:D - 1], c[:, 1:D - 1:D - 3], c[:, 1:D - 1:D - 3], ALU.add).then_inc(l0h, 1)
                dve.wait_ge(l0h, 2 * r + 2)
                lap(0, r)
            pick_c0(1)
            for e in PRE_EVENTS:
                if e[0] == "U":
                    up(PRE, e)
                else:
                    event(e, PRE)

            def body(it):
                if it.post:
                    moments(it, it.l - 1, bank=0)
                if it.lzero:
                    pick_c0(it.m + 1)
                lo(it, 0)
                for c in range(FC):
                    with_up = has_up(it, c)
                    if not with_up:
                        add_h(it, c)
                        add_h2(it, c)
                    for e in it.slots[c]:
                        if e[0] == "U":
                            up(it, e, c)
                        else:
                            event(e, it)
                    if c + 1 < FC and not with_up:
                        lo(it, c + 1)

            iterations(dve, body)
            moments(LAST, L - 1, bank=0)
            for e in LAST_EVENTS:
                event(e, LAST)

        @block.tensor
        def _(pe):
            release = {}

            def take(it, e, who, count):
                b = it.bank[e]
                if b in release:
                    wait(pe, *release[b])
                release[b] = (who, count)
                return fp[:, b]

            def mm3(out_, lhs, rhs, pairs, done=None):
                n = len(pairs)
                for q, (a, b) in enumerate(pairs):
                    for t, (u, v) in enumerate(((0, 0), (0, 1), (1, 0))):
                        last = pe.matmul(out_, lhs(u, a), rhs(v, b), start=(q == 0 and t == 0),
                                         stop=(q == n - 1 and t == 2))
                if done is not None:
                    last.then_inc(done, 1)

            def turn(bank, src, done):
                for k in range(NT):
                    last = pe.transpose(bank[:, k * P:(k + 1) * P], src(k), ident[:, :])
                last.then_inc(done, 1)

            ks = [(k, k) for k in range(NT)]

            def up_chunk(l, c):
                n = l * FC + c
                if c == 0:
                    pe.wait_ge(tlo_done, l * 12 + 12)
                    if isinstance(l, int):
                        pe.wait_ge(s_w1l, NT)
                wait(pe, sum_done, n - 1)
                mm3(hp[:, c % 2], lambda u, k: w1s[:, u, k, c * P:(c + 1) * P], lambda v, k: x3t[:, v, k], ks, w1_done)

            def down_tile(it, c, j):
                n = it.l * FC + c
                if j == 0:
                    pe.wait_ge(lo_done, n + 1)
                    if PREPARE_0 in it.more:
                        pe.wait_ge(s_wsl, c + 1)
                if c == 0 and it.post:
                    pe.wait_ge(y2_done, (it.l - 1) * NT + j + 1)
                for t, (u, v) in enumerate(((0, 0), (0, 1), (1, 0))):
                    last = pe.matmul(phi[:, j], hs[:, c % 2, u, j * P:(j + 1) * P], w2s[:, v, c],
                                     start=(c == 0 and t == 0), stop=(c == FC - 1 and t == 2))
                if c == FC - 1:
                    last.then_inc(phi_done, 1)
                elif j == NT - 1:
                    last.then_inc(w2_done, 1)

            def event(e, it):
                m = it.m
                if e[0] == "CS":
                    c = e[1]
                    if c == 0:
                        pe.wait_ge(s_small, 8 * 16)
                    if c % NT == 0:
                        pe.wait_ge(s_w2ld[c // NT], 16)
                    mm = pe.matmul(phi[0:2, 0], bg1[:, c], w2_raw[c], start=(c == 0), stop=(c == FC - 1))
                    if c == FC - 1:
                        mm.then_inc(s_csum, 1)
                if e[0] == "CB":
                    pe.wait_ge(s_cs, 1)
                    for n in range(2):
                        mm = pe.matmul(phi[:, 1 + n], ident[0:2, n:n + 1].to_broadcast([2, P]), sums,
                                       start=True, stop=True)
                    mm.then_inc(s_csum, 1)
                if e[0] == "T":
                    t, j = e[1:]
                    i = m * 12 + 4 * t + j
                    if t == 0:
                        pe.wait_ge(l0x, m * NT + j + 1)
                    else:
                        pe.wait_ge(xn_done, m * 8 + NT * (t - 1) + j + 1)
                    src = x1[:, j] if t == 0 else xr[:, it.par, j]
                    turn(take(it, e, tlo_done, i + 1), lambda k: src[:, k * P:(k + 1) * P], tr_done)
                if e[0] == "D":
                    y_ = e[1]
                    w = m * 2 + y_
                    pe.wait_ge(tlo_done, m * 12 + 4 * y_ + NT)
                    pe.wait_ge(wc_lo, w + 1)
                    mm3(take(it, e, relu_done, w + 1), lambda u, k: ws[:, u, 0, k * BK:(k + 1) * BK],
                        lambda v, k: ft[:, v, k], ks, dn_done)
                if e[0] == "U":
                    y_, j = e[1:]
                    i = m * 8 + 4 * y_ + j
                    pe.wait_ge(zlo_done, m * 2 + y_ + 1)
                    mm3(take(it, e, yf_done, i + 1), lambda u, k: zs[:, u, j * P:(j + 1) * P],
                        lambda v, k: ws[:, v, 1], [(0, 0)], up_done)
                if e[0] == "CT":
                    j = e[1]
                    i = it.k * NT + j
                    pe.wait_ge(s_done, (it.l - 1) * NT + j + 1)
                    turn(take(it, e, clo_done, i + 1), lambda k: s[:, j, k * P:(k + 1) * P], ctr_done)
                if e[0] == "PC":
                    mm_ = e[1]
                    n = it.k * NT + mm_
                    pe.wait_ge(clo_done, it.k * NT + NT)
                    pe.wait_ge(wtl_done, n + 1)
                    who = (pe_done if it.mix == "P" else qa_done, it.cg * NT + mm_ + 1)
                    mm3(take(it, e, *who), lambda u, k: wts[:, u, k], lambda v, k: ct[:, v, k], ks, pc_done)
                if e[0] == "QP":
                    j = e[1]
                    pe.wait_ge(clo_done, it.k * NT + j + 1)
                    pe.wait_ge(wtl_done, it.k * NT + NT)
                    pe.wait_ge(y2_done, (it.l - 1) * NT + j + 1)
                    for n in range(NT):
                        mm3(phi[:, j, n * P:(n + 1) * P], lambda u, k: ft[:, u, n, k * P:(k + 1) * P],
                            lambda v, k: ct[:, v, k, j * P:(j + 1) * P], ks, pc_done if n == NT - 1 else None)
                if e[0] == "GT":
                    j = e[1]
                    i = it.cg * NT + j
                    if it is LAST:
                        pe.wait_ge(qp_done, (j + 1) * NT)
                    else:
                        pe.wait_ge(qg_done, it.cg * NT + NT)
                    turn(take(it, e, gy_done, i + 1), lambda k: pt[:, k, j * P:(j + 1) * P], gt_done)
                if e[0] == "ST":
                    n = it.l * FC + FC
                    pe.wait_ge(sum_done, n)
                    pe.wait_ge(sumsq_done, n)
                    bank = take(it, e, mom_done, it.l * 4 + 2)
                    for j in range(NT):
                        for w in range(2):
                            last = pe.matmul(bank[:, 2 * j + w:2 * j + w + 1], hsum[:, w, j * P:(j + 1) * P],
                                             ones[:, :], start=True, stop=True)
                    last.then_inc(stats_done, 1)

            pe.wait_ge(s_cst, 5)
            for e in PRE_EVENTS:
                event(e, PRE)

            def body(it):
                if it.post:
                    release.clear()
                    release[0] = (mom_done, it.l * 4 - 2)
                    release[1] = (tlo_done, it.l * 12 + 12)
                up_chunk(it.l, 0)
                for c in range(FC - 1):
                    for e in it.slots[c]:
                        if e[0] in EARLY:
                            event(e, it)
                    up_chunk(it.l, c + 1)
                    for e in it.slots[c]:
                        if e[0] not in EARLY:
                            event(e, it)
                    for j in range(NT):
                        down_tile(it, c, j)
                turns = [e for e in it.slots[FC - 1] if e[0] in USES_F]
                for e in turns[:1]:
                    event(e, it)
                for j in range(NT):
                    if j == NT - 1:
                        event(("ST",), it)
                    down_tile(it, FC - 1, j)
                    if j >= 1 and j < len(turns):
                        event(turns[j], it)

            iterations(pe, body)
            release.clear()
            release[0] = (mom_done, L * 4 - 2)
            for e in LAST_EVENTS:
                event(e, LAST)


_INS = ['x', 'condB_zX', 'condB_zY', 'condB_zR', 'itok_B_0_6', 'itok_B_0_8', 'condB_alphaparams',
        'L1_cond_down_w', 'L1_cond_down_b', 'L1_cond_up_w', 'L1_cond_up_b', 'L1_cond_ln_g', 'L1_cond_ln_b',
        'L2_cond_W1', 'L2_cond_b1', 'L2_cond_W2', 'L2_cond_b2', 'L2_cond_gamma', 'L2_cond_beta',
        'L3_cond_s_init', 'L3_cond_W1', 'L3_cond_b1', 'L3_cond_g1', 'L3_cond_be1', 'L3_cond_W2', 'L3_cond_b2',
        'L3_cond_g2', 'L3_cond_be2', 'L3_cond_Wt', 'L3_cond_bt', 'L3_cond_gt', 'L3_cond_bet']


def kernel(**inputs):
    import numpy as np
    import concourse.bacc as bacc
    from concourse.bass_utils import run_bass_kernel_spmd

    nc = bacc.Bacc("TRN2", target_bir_lowering=False, num_devices=1)
    arrays, args = {}, []
    for name in _INS:
        a = np.ascontiguousarray(inputs[name])
        arrays[f"in_{name}"] = a
        args.append(nc.dram_tensor(f"in_{name}", a.shape, mybir.dt.from_np(a.dtype), kind="ExternalInput").ap())
    args.append(nc.dram_tensor("out_0", (L, D, D), F32, kind="ExternalOutput").ap())
    build(nc, *args)
    r = run_bass_kernel_spmd(nc, [arrays], core_ids=[0])
    return r.results[0]["out_0"]
```
